# Optimizing a Trainium2 kernel written in Bass

```python
import numpy as np
import jax
import jax.numpy as jnp

def _softmax(x, axis=-1):
    return jax.nn.softmax(x, axis=axis)

def _gelu(x):
    return jax.nn.gelu(x, approximate=True)

def _silu(x):
    return jax.nn.silu(x)

def _sigmoid(x):
    return jax.nn.sigmoid(x)

def _layernorm(x, axis=-1, eps=1e-05):
    m = jnp.mean(x, axis=axis, keepdims=True)
    v = jnp.var(x, axis=axis, keepdims=True)
    return (x - m) / jnp.sqrt(v + eps)

def _scatter_add(tgt, idx, src, axis=0):
    return tgt.at[idx].add(src)

def _segment_sum(src, seg, n):
    return jax.ops.segment_sum(src, seg, n)
kernel_name = 'mk_xattn_seq_d2_seqx_r8_fb2a8a'

def setup_inputs(seed: int=0):
    np.random.seed(seed)
    _w = jnp.asarray

    def _rec_inputs():
        import jax
        import jax.numpy as jnp
        _rk = jax.random.key(seed)
        x = 7.22e-05 + 1 * jax.random.normal(jax.random.fold_in(_rk, 1), (128, 64, 128), jnp.float32)
        _lenS = 64 - jax.random.randint(jax.random.fold_in(_rk, 7), (128,), 0, max(1, 64 // 4) + 1, jnp.int32)
        _lenS2 = 64 - jax.random.randint(jax.random.fold_in(_rk, 8), (128,), 0, max(1, 64 // 4) + 1, jnp.int32)
        _ctx_1024P = jax.random.normal(jax.random.fold_in(_rk, 11), (128, 16, 128), jnp.float32)
        _ctx_1024c = jax.random.dirichlet(jax.random.fold_in(_rk, 511), 0.3 * jnp.ones((16,), jnp.float32), (128, 64))
        _ctx_1024t = jnp.einsum('bsk,bkd->bsd', _ctx_1024c, _ctx_1024P)
        _ctx_1024t = _ctx_1024t * jax.lax.rsqrt(jnp.mean(jnp.square(_ctx_1024t)) + 1e-12) * 0.953939
        ctx_1024 = 4.13588e-05 + 0.999923 * (_ctx_1024t + 0.3 * jax.random.normal(jax.random.fold_in(_rk, 611), (128, 64, 128), jnp.float32))
        _validS = jnp.arange(64)[None, :] < _lenS[:, None]
        _validS2 = jnp.arange(64)[None, :] < _lenS2[:, None]
        _causal = jnp.tril(jnp.ones((64, 64), dtype=bool))
        mask_BxS2_ik0 = jnp.where(jnp.broadcast_to(_validS2[:, :], (128, 64)), 0, 1).astype(jnp.int32)
        return (x, ctx_1024, mask_BxS2_ik0)
    x, ctx_1024, mask_BxS2_ik0 = _rec_inputs()

    def _L0_xattn_setup():
        import jax, jax.numpy as jnp
        import numpy as np
        H = 16
        EPS = 1e-05
        key = jax.random.key(seed)
        ks = jax.random.split(key, 12)
        B, S, D = (4, 256, 128)
        sc = 1.0 / np.sqrt(D)
        return {'queries': jax.random.normal(ks[0], (B, S, D), jnp.float32), 'keys': jax.random.normal(ks[1], (B, S, D), jnp.float32), 'values': jax.random.normal(ks[2], (B, S, D), jnp.float32), 'attention_mask': jax.random.randint(ks[3], (B, S), 0, 2, jnp.int32), 'Wq': jax.random.normal(ks[4], (D, D), jnp.float32) * sc, 'bq': jnp.zeros((D,), jnp.float32), 'Wk': jax.random.normal(ks[5], (D, D), jnp.float32) * sc, 'bk': jnp.zeros((D,), jnp.float32), 'Wv': jax.random.normal(ks[6], (D, D), jnp.float32) * sc, 'bv': jnp.zeros((D,), jnp.float32), 'gamma': jnp.ones((D,), jnp.float32), 'beta': jnp.zeros((D,), jnp.float32)}
    _L0_xattn_all = _L0_xattn_setup()
    _L0_xattn_in = {k: v for k, v in _L0_xattn_all.items() if k in ('Wq', 'bq', 'Wk', 'bk', 'Wv', 'bv', 'gamma', 'beta')}
    del _L0_xattn_all

    def _L1_xattn_setup():
        import jax, jax.numpy as jnp
        import numpy as np
        import math
        D_MODEL = 128
        NUM_HEADS = 16
        D_FF = 512
        EPS = 1e-05

        def _linear_params(key, fan_in, fan_out):
            k1, k2 = jax.random.split(key)
            bound = 1.0 / math.sqrt(fan_in)
            W = jax.random.uniform(k1, (fan_in, fan_out), jnp.float32, -bound, bound)
            b = jax.random.uniform(k2, (fan_out,), jnp.float32, -bound, bound)
            return (W, b)

        def _layernorm(x, g, b):
            mu = jnp.mean(x, axis=-1, keepdims=True)
            var = jnp.mean((x - mu) ** 2, axis=-1, keepdims=True)
            return (x - mu) * jax.lax.rsqrt(var + EPS) * g + b

        def _mha(q_in, kv_in, wq, bq, wk, bk, wv, bv, wo, bo):
            B, Sq, D = q_in.shape
            Skv = kv_in.shape[1]
            H, dk = (NUM_HEADS, D // NUM_HEADS)
            Q = (q_in @ wq + bq).reshape(B, Sq, H, dk).transpose(0, 2, 1, 3)
            K = (kv_in @ wk + bk).reshape(B, Skv, H, dk).transpose(0, 2, 1, 3)
            V = (kv_in @ wv + bv).reshape(B, Skv, H, dk).transpose(0, 2, 1, 3)
            scores = jnp.einsum('bhqd,bhkd->bhqk', Q, K) / math.sqrt(dk)
            probs = jax.nn.softmax(scores, axis=-1)
            attn = jnp.einsum('bhqk,bhkd->bhqd', probs, V)
            attn = attn.transpose(0, 2, 1, 3).reshape(B, Sq, D)
            return attn @ wo + bo
        key = jax.random.key(seed)
        keys = jax.random.split(key, 16)
        src = jax.random.normal(keys[0], (4, 256, D_MODEL), jnp.float32)
        tgt = jax.random.normal(keys[1], (4, 256, D_MODEL), jnp.float32)
        sa_wq, sa_bq = _linear_params(keys[2], D_MODEL, D_MODEL)
        sa_wk, sa_bk = _linear_params(keys[3], D_MODEL, D_MODEL)
        sa_wv, sa_bv = _linear_params(keys[4], D_MODEL, D_MODEL)
        sa_wo, sa_bo = _linear_params(keys[5], D_MODEL, D_MODEL)
        ca_wq, ca_bq = _linear_params(keys[6], D_MODEL, D_MODEL)
        ca_wk, ca_bk = _linear_params(keys[7], D_MODEL, D_MODEL)
        ca_wv, ca_bv = _linear_params(keys[8], D_MODEL, D_MODEL)
        ca_wo, ca_bo = _linear_params(keys[9], D_MODEL, D_MODEL)
        ff_w1, ff_b1 = _linear_params(keys[10], D_MODEL, D_FF)
        ff_w2, ff_b2 = _linear_params(keys[11], D_FF, D_MODEL)
        ones = jnp.ones((D_MODEL,), jnp.float32)
        zeros = jnp.zeros((D_MODEL,), jnp.float32)
        return dict(src=src, tgt=tgt, sa_wq=sa_wq, sa_bq=sa_bq, sa_wk=sa_wk, sa_bk=sa_bk, sa_wv=sa_wv, sa_bv=sa_bv, sa_wo=sa_wo, sa_bo=sa_bo, ca_wq=ca_wq, ca_bq=ca_bq, ca_wk=ca_wk, ca_bk=ca_bk, ca_wv=ca_wv, ca_bv=ca_bv, ca_wo=ca_wo, ca_bo=ca_bo, ff_w1=ff_w1, ff_b1=ff_b1, ff_w2=ff_w2, ff_b2=ff_b2, ln1_g=ones, ln1_b=zeros, ln2_g=ones, ln2_b=zeros, ln3_g=ones, ln3_b=zeros)
    _L1_xattn_all = _L1_xattn_setup()
    _L1_xattn_in = {k: v for k, v in _L1_xattn_all.items() if k in ('sa_wq', 'sa_bq', 'sa_wk', 'sa_bk', 'sa_wv', 'sa_bv', 'sa_wo', 'sa_bo', 'ca_wq', 'ca_bq', 'ca_wk', 'ca_bk', 'ca_wv', 'ca_bv', 'ca_wo', 'ca_bo', 'ff_w1', 'ff_b1', 'ff_w2', 'ff_b2', 'ln1_g', 'ln1_b', 'ln2_g', 'ln2_b', 'ln3_g', 'ln3_b')}
    del _L1_xattn_all
    return {'x': x, 'ctx_1024': ctx_1024, 'mask_BxS2_ik0': mask_BxS2_ik0, 'L0_xattn_Wq': _L0_xattn_in['Wq'], 'L0_xattn_bq': _L0_xattn_in['bq'], 'L0_xattn_Wk': _L0_xattn_in['Wk'], 'L0_xattn_bk': _L0_xattn_in['bk'], 'L0_xattn_Wv': _L0_xattn_in['Wv'], 'L0_xattn_bv': _L0_xattn_in['bv'], 'L0_xattn_gamma': _L0_xattn_in['gamma'], 'L0_xattn_beta': _L0_xattn_in['beta'], 'L1_xattn_sa_wq': _L1_xattn_in['sa_wq'], 'L1_xattn_sa_bq': _L1_xattn_in['sa_bq'], 'L1_xattn_sa_wk': _L1_xattn_in['sa_wk'], 'L1_xattn_sa_bk': _L1_xattn_in['sa_bk'], 'L1_xattn_sa_wv': _L1_xattn_in['sa_wv'], 'L1_xattn_sa_bv': _L1_xattn_in['sa_bv'], 'L1_xattn_sa_wo': _L1_xattn_in['sa_wo'], 'L1_xattn_sa_bo': _L1_xattn_in['sa_bo'], 'L1_xattn_ca_wq': _L1_xattn_in['ca_wq'], 'L1_xattn_ca_bq': _L1_xattn_in['ca_bq'], 'L1_xattn_ca_wk': _L1_xattn_in['ca_wk'], 'L1_xattn_ca_bk': _L1_xattn_in['ca_bk'], 'L1_xattn_ca_wv': _L1_xattn_in['ca_wv'], 'L1_xattn_ca_bv': _L1_xattn_in['ca_bv'], 'L1_xattn_ca_wo': _L1_xattn_in['ca_wo'], 'L1_xattn_ca_bo': _L1_xattn_in['ca_bo'], 'L1_xattn_ff_w1': _L1_xattn_in['ff_w1'], 'L1_xattn_ff_b1': _L1_xattn_in['ff_b1'], 'L1_xattn_ff_w2': _L1_xattn_in['ff_w2'], 'L1_xattn_ff_b2': _L1_xattn_in['ff_b2'], 'L1_xattn_ln1_g': _L1_xattn_in['ln1_g'], 'L1_xattn_ln1_b': _L1_xattn_in['ln1_b'], 'L1_xattn_ln2_g': _L1_xattn_in['ln2_g'], 'L1_xattn_ln2_b': _L1_xattn_in['ln2_b'], 'L1_xattn_ln3_g': _L1_xattn_in['ln3_g'], 'L1_xattn_ln3_b': _L1_xattn_in['ln3_b']}

def reference(x, ctx_1024, mask_BxS2_ik0, L0_xattn_Wq, L0_xattn_bq, L0_xattn_Wk, L0_xattn_bk, L0_xattn_Wv, L0_xattn_bv, L0_xattn_gamma, L0_xattn_beta, L1_xattn_sa_wq, L1_xattn_sa_bq, L1_xattn_sa_wk, L1_xattn_sa_bk, L1_xattn_sa_wv, L1_xattn_sa_bv, L1_xattn_sa_wo, L1_xattn_sa_bo, L1_xattn_ca_wq, L1_xattn_ca_bq, L1_xattn_ca_wk, L1_xattn_ca_bk, L1_xattn_ca_wv, L1_xattn_ca_bv, L1_xattn_ca_wo, L1_xattn_ca_bo, L1_xattn_ff_w1, L1_xattn_ff_b1, L1_xattn_ff_w2, L1_xattn_ff_b2, L1_xattn_ln1_g, L1_xattn_ln1_b, L1_xattn_ln2_g, L1_xattn_ln2_b, L1_xattn_ln3_g, L1_xattn_ln3_b):
    import jax
    import jax.numpy as jnp

    def _L0_xattn_ref(queries, keys, values, attention_mask, Wq, bq, Wk, bk, Wv, bv, gamma, beta):
        import jax, jax.numpy as jnp
        import numpy as np
        H = 16
        EPS = 1e-05
        B, S, D = queries.shape
        dh = D // H
        q = jax.nn.relu(jnp.einsum('bsd,de->bse', queries, Wq) + bq)
        k = jax.nn.relu(jnp.einsum('bsd,de->bse', keys, Wk) + bk)
        v = jax.nn.relu(jnp.einsum('bsd,de->bse', values, Wv) + bv)
        q_ = q.reshape(B, S, H, dh).transpose(0, 2, 1, 3)
        k_ = k.reshape(B, S, H, dh).transpose(0, 2, 1, 3)
        v_ = v.reshape(B, S, H, dh).transpose(0, 2, 1, 3)
        scores = jnp.einsum('bhqd,bhkd->bhqk', q_, k_) / jnp.sqrt(jnp.float32(dh))
        m = attention_mask[:, None, :, None].astype(bool)
        scores = jnp.where(m, scores, jnp.float32(1e-09))
        a = jax.nn.softmax(scores, axis=-1)
        o = jnp.einsum('bhqk,bhkd->bhqd', a, v_)
        o = o.transpose(0, 2, 1, 3).reshape(B, S, D)
        x = o + queries
        mu = jnp.mean(x, axis=-1, keepdims=True)
        var = jnp.mean(jnp.square(x - mu), axis=-1, keepdims=True)
        return (x - mu) * jax.lax.rsqrt(var + EPS) * gamma + beta

    def _L1_xattn_ref(src, tgt, sa_wq, sa_bq, sa_wk, sa_bk, sa_wv, sa_bv, sa_wo, sa_bo, ca_wq, ca_bq, ca_wk, ca_bk, ca_wv, ca_bv, ca_wo, ca_bo, ff_w1, ff_b1, ff_w2, ff_b2, ln1_g, ln1_b, ln2_g, ln2_b, ln3_g, ln3_b):
        import jax, jax.numpy as jnp
        import numpy as np
        import math
        D_MODEL = 128
        NUM_HEADS = 16
        D_FF = 512
        EPS = 1e-05

        def _linear_params(key, fan_in, fan_out):
            k1, k2 = jax.random.split(key)
            bound = 1.0 / math.sqrt(fan_in)
            W = jax.random.uniform(k1, (fan_in, fan_out), jnp.float32, -bound, bound)
            b = jax.random.uniform(k2, (fan_out,), jnp.float32, -bound, bound)
            return (W, b)

        def _layernorm(x, g, b):
            mu = jnp.mean(x, axis=-1, keepdims=True)
            var = jnp.mean((x - mu) ** 2, axis=-1, keepdims=True)
            return (x - mu) * jax.lax.rsqrt(var + EPS) * g + b

        def _mha(q_in, kv_in, wq, bq, wk, bk, wv, bv, wo, bo):
            B, Sq, D = q_in.shape
            Skv = kv_in.shape[1]
            H, dk = (NUM_HEADS, D // NUM_HEADS)
            Q = (q_in @ wq + bq).reshape(B, Sq, H, dk).transpose(0, 2, 1, 3)
            K = (kv_in @ wk + bk).reshape(B, Skv, H, dk).transpose(0, 2, 1, 3)
            V = (kv_in @ wv + bv).reshape(B, Skv, H, dk).transpose(0, 2, 1, 3)
            scores = jnp.einsum('bhqd,bhkd->bhqk', Q, K) / math.sqrt(dk)
            probs = jax.nn.softmax(scores, axis=-1)
            attn = jnp.einsum('bhqk,bhkd->bhqd', probs, V)
            attn = attn.transpose(0, 2, 1, 3).reshape(B, Sq, D)
            return attn @ wo + bo
        sa = _mha(tgt, tgt, sa_wq, sa_bq, sa_wk, sa_bk, sa_wv, sa_bv, sa_wo, sa_bo)
        x = _layernorm(tgt + sa, ln1_g, ln1_b)
        ca = _mha(x, src, ca_wq, ca_bq, ca_wk, ca_bk, ca_wv, ca_bv, ca_wo, ca_bo)
        x = _layernorm(x + ca, ln2_g, ln2_b)
        ff = jax.nn.relu(x @ ff_w1 + ff_b1) @ ff_w2 + ff_b2
        x = _layernorm(x + ff, ln3_g, ln3_b)
        return x
    x = _L0_xattn_ref(x, ctx_1024, ctx_1024, mask_BxS2_ik0, L0_xattn_Wq, L0_xattn_bq, L0_xattn_Wk, L0_xattn_bk, L0_xattn_Wv, L0_xattn_bv, L0_xattn_gamma, L0_xattn_beta)
    x = _L1_xattn_ref(ctx_1024, x, L1_xattn_sa_wq, L1_xattn_sa_bq, L1_xattn_sa_wk, L1_xattn_sa_bk, L1_xattn_sa_wv, L1_xattn_sa_bv, L1_xattn_sa_wo, L1_xattn_sa_bo, L1_xattn_ca_wq, L1_xattn_ca_bq, L1_xattn_ca_wk, L1_xattn_ca_bk, L1_xattn_ca_wv, L1_xattn_ca_bv, L1_xattn_ca_wo, L1_xattn_ca_bo, L1_xattn_ff_w1, L1_xattn_ff_b1, L1_xattn_ff_w2, L1_xattn_ff_b2, L1_xattn_ln1_g, L1_xattn_ln1_b, L1_xattn_ln2_g, L1_xattn_ln2_b, L1_xattn_ln3_g, L1_xattn_ln3_b)
    return x

_drawn_inputs = setup_inputs


def setup_inputs(seed=0):
    import zlib

    import numpy as np

    out = dict(_drawn_inputs(seed))
    spreads = {'L0_xattn_bq': (0.0, 2.0),
     'L0_xattn_bk': (0.0, 0.8),
     'L0_xattn_bv': (0.0, 0.1),
     'L0_xattn_gamma': (1.0, 0.2),
     'L0_xattn_beta': (0.0, 0.1),
     'L1_xattn_ln1_g': (1.0, 0.2),
     'L1_xattn_ln1_b': (0.0, 0.1),
     'L1_xattn_ln2_g': (1.0, 0.2),
     'L1_xattn_ln2_b': (0.0, 0.1),
     'L1_xattn_ln3_g': (1.0, 0.2),
     'L1_xattn_ln3_b': (0.0, 0.1)}
    factors = {'L0_xattn_Wq': 2.942,
     'L1_xattn_sa_wq': 3.47,
     'L1_xattn_sa_bq': 8.0,
     'L1_xattn_sa_wk': 3.411,
     'L1_xattn_sa_bk': 64.0,
     'L1_xattn_ca_bq': 31.816,
     'L1_xattn_ca_bk': 64.0,
     'L1_xattn_ff_b1': 3.054}
    for name, (base, spread) in spreads.items():
        noise = np.random.default_rng([zlib.crc32(name.encode()), seed]).standard_normal(out[name].shape)
        drawn = base * np.exp(spread * noise) if base else spread * noise
        out[name] = jnp.asarray(drawn.astype(out[name].dtype))
    for name, factor in factors.items():
        out[name] = (out[name] * factor).astype(out[name].dtype)
    return out
```

```python
from contextlib import ExitStack

import numpy as np

import concourse.bass as bass
from concourse import mybir

F32 = mybir.dt.float32
ALU = mybir.AluOpType
ACT = mybir.ActivationFunctionType
AX = mybir.AxisListType

B, S, D, H, FF = 128, 64, 128, 16, 512
DH = D // H
P = 128
TILES = B * S // P
LAYERS = 3
G = LAYERS * TILES
HALF = H // 2
PAIRS = HALF // 2
VC = 2 * DH
EPS = 1e-5
SCALE = float(1.0 / np.sqrt(np.float32(DH)))
SLOTS = 4
FCH = FF // P
GROUP = 4
GROUPS = TILES // GROUP
SELF, CROSS = 1, 2


class At:

    def __init__(self, n, stride, r=None):
        self.n, self.stride, self.r = n, stride, r

    def __add__(self, k):
        return At(self.n + k, self.stride, self.r)

    def __sub__(self, k):
        return At(self.n - k, self.stride, self.r)

    def value(self, k=0):
        return self.n + k if self.r is None else self.r * self.stride + (self.n + k)

    def rounds(self, k=0):
        n = (self.n - k) // self.stride
        return 16 * n if self.r is None else self.r * 16 + 16 * n

    @property
    def layer(self):
        return self.n // TILES

    @property
    def slot(self):
        return self.n % SLOTS

    @property
    def par(self):
        return self.n % 2


def due(count):
    return not isinstance(count, int) or count >= 1


def walk_tiles(eng, step, before, after):
    for n in range(-before, 2 * SLOTS):
        step(At(n, SLOTS))
    for layer in range(LAYERS):
        first, last = layer * TILES + 2 * SLOTS, (layer + 1) * TILES - 2 * SLOTS
        with eng.Fori(0, (last - first) // SLOTS) as r:
            for k in range(SLOTS):
                step(At(first + k, SLOTS, r))
        end = G + after if layer == LAYERS - 1 else (layer + 1) * TILES + 2 * SLOTS
        for n in range(last, end):
            step(At(n, SLOTS))


def walk_groups(eng, step, before, after):
    for n in range(-before, 4):
        step(At(n, 2))
    with eng.Fori(0, (GROUPS - 8) // 2) as r:
        for k in range(2):
            step(At(4 + k, 2, r))
    for n in range(GROUPS - 4, GROUPS + after):
        step(At(n, 2))


def exists(g):
    return 0 <= g.n < G


def group_exists(j):
    return 0 <= j.n < GROUPS


def build(nc, a, out, mid):
    ctx = ExitStack()
    with ctx:
        def sb(name, shape, dt=F32):
            return ctx.enter_context(nc.sbuf_tensor(name, shape, dt))

        def bank(name):
            return ctx.enter_context(nc.psum_tensor(name, [P, 512], F32))

        def sem(name):
            return ctx.enter_context(nc.semaphore(name))

        ident = sb("ident", [P, P])
        head_mask = sb("head_mask", [P, H])
        neg_half = sb("neg_half", [P, GROUP])
        w_q = sb("w_q", [P, LAYERS, D])
        w_k = sb("w_k", [P, LAYERS, D])
        w_v = sb("w_v", [P, LAYERS, D])
        w_o = sb("w_o", [P, LAYERS, D])
        b_q = sb("b_q", [P, LAYERS])
        b_k = sb("b_k", [P, LAYERS])
        b_v = sb("b_v", [P, LAYERS, H // 2, DH])
        b_o = sb("b_o", [P, LAYERS, D])
        ln_g = sb("ln_g", [P, LAYERS + 1, D])
        ln_b = sb("ln_b", [P, LAYERS + 1, D])
        w_1 = sb("w_1", [P, FF])
        b_1 = sb("b_1", [P, FCH])
        w_2 = sb("w_2", [P, FCH, D])
        b_2 = sb("b_2", [P, D])
        mask_i = sb("mask_i", [P, TILES], mybir.dt.int32)
        mask_f = sb("mask_f", [P, TILES])
        row_scale = sb("row_scale", [P, TILES])

        x_in = sb("x_in", [P, SLOTS, D])
        c_in = sb("c_in", [P, SLOTS, D])
        x_res = sb("x_res", [P, SLOTS, D])
        xcT = sb("xcT", [P, SLOTS, 2, P])
        QT = sb("QT", [P, SLOTS, P])
        KT = sb("KT", [P, SLOTS, P])
        Kx = sb("Kx", [P, 2, 2, H, S])
        v_sum = sb("v_sum", [P, 2, H // 2, DH])
        Vx = sb("Vx", [P, SLOTS, 2, H // 2, 2, VC])
        row_max = sb("row_max", [P, 2, H])
        shifted = sb("shifted", [P, 2, 2, HALF, S])
        probs = sb("probs", [P, 2, 2, HALF * S])
        PT = sb("PT", [P, 2, 2, PAIRS, P])
        OT = sb("OT", [P, 2, 2, P])
        inv_sum = sb("inv_sum", [P, 2, H])
        attn = sb("attn", [P, 2, H, DH])
        attnT = sb("attnT", [P, 2, P])
        y_x = sb("y_x", [P, D])
        z = sb("z", [P, SLOTS, D])
        stats = sb("stats", [P, 6])
        mean_var = sb("mean_var", [P, SLOTS, 2])
        var_eps = sb("var_eps", [P, SLOTS])
        rstd = sb("rstd", [P, SLOTS])
        normed = sb("normed", [P, SLOTS, D])
        scaled = sb("scaled", [P, D])
        x_out = sb("x_out", [P, SLOTS, D])

        f_in = sb("f_in", [P, 2, GROUP, D])
        f_inT = sb("f_inT", [P, 2, GROUP * P])
        hidT = sb("hidT", [P, 2, FCH, GROUP * P])
        f_y = sb("f_y", [P, GROUP, D])
        f_z = sb("f_z", [P, 2, GROUP, D])
        f_stats = sb("f_stats", [P, GROUP, 6])
        f_mv = sb("f_mv", [P, 2, GROUP, 2])
        f_ve = sb("f_ve", [P, 2, GROUP])
        f_rstd = sb("f_rstd", [P, 2, GROUP])
        f_norm = sb("f_norm", [P, 2, GROUP, D])
        f_scaled = sb("f_scaled", [P, GROUP, D])
        f_out = sb("f_out", [P, 2, GROUP, D])

        in_bank = bank("in_bank")
        proj_bank = bank("proj_bank")
        score_bank = [bank("score_bank0"), bank("score_bank1")]
        pt_bank = [bank("pt_bank0"), bank("pt_bank1")]
        ot_bank = bank("ot_bank")
        tail_bank = bank("tail_bank")

        loaded = sem("loaded")
        consts_zero = sem("consts_zero")
        consts_band = sem("consts_band")
        consts_set = sem("consts_set")
        mask_cast = sem("mask_cast")
        mask_set = sem("mask_set")
        v_zeroed = sem("v_zeroed")
        v_ones = sem("v_ones")
        x_loaded = [sem(f"x_loaded{s}") for s in range(SLOTS)]
        c_loaded = [sem(f"c_loaded{s}") for s in range(SLOTS)]
        res_loaded = [sem(f"res_loaded{s}") for s in range(SLOTS)]
        stored = [sem(f"stored{s}") for s in range(SLOTS)]
        in_transposed = sem("in_transposed")
        in_copied = sem("in_copied")
        projected = sem("projected")
        k_ready = sem("k_ready")
        q_ready = sem("q_ready")
        v_added = sem("v_added")
        v_ready = sem("v_ready")
        k_spread = sem("k_spread")
        scored = [sem("scored0"), sem("scored1")]
        max_ready = [sem("max_ready0"), sem("max_ready1")]
        shift_ready = [sem("shift_ready0"), sem("shift_ready1")]
        exp_ready = [sem("exp_ready0"), sem("exp_ready1")]
        probs_transposed = [sem("probs_transposed0"), sem("probs_transposed1")]
        pt_copied = [sem("pt_copied0"), sem("pt_copied1")]
        pv_done = sem("pv_done")
        ot_copied = sem("ot_copied")
        o_back = sem("o_back")
        inv_ready = sem("inv_ready")
        attn_ready = sem("attn_ready")
        attn_transposed = sem("attn_transposed")
        attn_copied = sem("attn_copied")
        y_done = sem("y_done")
        tail_free = sem("tail_free")
        z_ready = sem("z_ready")
        stats_ready = sem("stats_ready")
        mean_ready = sem("mean_ready")
        var_ready = sem("var_ready")
        rstd_ready = sem("rstd_ready")
        norm_ready = sem("norm_ready")
        gamma_done = sem("gamma_done")
        out_ready = sem("out_ready")
        f_loaded = [sem("f_loaded0"), sem("f_loaded1")]
        f_stored = [sem("f_stored0"), sem("f_stored1")]
        f_transposed = sem("f_transposed")
        f_copied = sem("f_copied")
        hid_done = [sem(f"hid_done{c}") for c in range(FCH)]
        hid_ready = [sem(f"hid_ready{c}") for c in range(FCH)]
        f_y_done = sem("f_y_done")
        f_y_read = sem("f_y_read")
        f_z_ready = sem("f_z_ready")
        f_stats_ready = sem("f_stats_ready")
        f_mean_ready = sem("f_mean_ready")
        f_var_ready = sem("f_var_ready")
        f_rstd_ready = sem("f_rstd_ready")
        f_norm_ready = sem("f_norm_ready")
        f_gamma_done = sem("f_gamma_done")
        f_out_ready = sem("f_out_ready")

        block = ctx.enter_context(nc.Block())

        def tiles_of(t):
            return t.rearrange("(t p) d -> t p d", p=P)

        x_t, c_t, out_t = tiles_of(a["x"]), tiles_of(a["ctx_1024"]), tiles_of(out)
        mid_t = [tiles_of(m) for m in mid]

        def tile_of(t, i):
            return t[i, :, :] if isinstance(i, int) else t[bass.ds(i, 1), :, :].rearrange("t p d -> (t p) d")

        def group_of(t, i):
            v = t.rearrange("(j t) p d -> j p t d", t=GROUP)
            return v[i] if isinstance(i, int) else v[bass.ds(i, 1)].rearrange("j p t d -> (j p) t d")

        def column(v, n):
            return v.rearrange("(c p) -> p c", p=n)

        def row(v):
            return v.rearrange("(a n) -> a n", a=1).to_broadcast([P, v.shape[0]])

        L1 = "L1_xattn_"
        kinds = ["L0_xattn_W", L1 + "sa_w", L1 + "ca_w"]
        biases = ["L0_xattn_b", L1 + "sa_b", L1 + "ca_b"]
        loads = []
        for n in range(LAYERS):
            loads += [(w_q[:, n, :], a[kinds[n] + "q"]), (w_k[:, n, :], a[kinds[n] + "k"]),
                      (w_v[:, n, :], a[kinds[n] + "v"]),
                      (b_q[:, n:n + 1], column(a[biases[n] + "q"], P)),
                      (b_k[:, n:n + 1], column(a[biases[n] + "k"], P))]
            for e in range(2):
                of_heads = a[biases[n] + "v"].rearrange("(c e d) -> e c d", e=2, d=DH)[e:e + 1, :, :]
                loads.append((b_v[e * S:(e + 1) * S, n, :, :], of_heads.to_broadcast([S, H // 2, DH])))
            if n:
                loads += [(w_o[:, n, :], a[kinds[n] + "o"]), (b_o[:, n, :], row(a[biases[n] + "o"]))]
        for n, (g, b) in enumerate([("L0_xattn_gamma", "L0_xattn_beta")] +
                                   [(L1 + f"ln{i}_g", L1 + f"ln{i}_b") for i in (1, 2, 3)]):
            loads += [(ln_g[:, n, :], row(a[g])), (ln_b[:, n, :], row(a[b]))]
        loads += [(w_1[:, :], a[L1 + "ff_w1"]), (b_1[:, :], column(a[L1 + "ff_b1"], P)),
                  (w_2[:, :, :], a[L1 + "ff_w2"].rearrange("(c p) n -> p c n", p=P)),
                  (b_2[:, :], row(a[L1 + "ff_b2"])),
                  (mask_i[:, :], a["mask_BxS2_ik0"].rearrange("(t b) s -> (b s) t", b=P // S))]
        LOADED = 16 * len(loads)

        @block.sync
        def _(sp):
            def weights_loaded(g):
                if g.r is not None:
                    sp.wait_ge(loaded, LOADED)

            def load_inputs(g):
                weights_loaded(g)
                if due(g.value(1 - SLOTS)):
                    sp.wait_ge(in_transposed, g.value(1 - SLOTS))
                src, tile = x_t if g.layer == 0 else mid_t[g.layer - 1], g.value(-g.layer * TILES)
                sp.dma_start(x_in[:, g.slot, :], tile_of(src, tile)).then_inc(x_loaded[g.slot], 16)
                if g.layer != SELF:
                    sp.dma_start(c_in[:, g.slot, :], tile_of(c_t, tile)).then_inc(c_loaded[g.slot], 16)

            def load_residual(g):
                weights_loaded(g)
                if due(g.value(1 - SLOTS)):
                    sp.wait_ge(z_ready, g.value(1 - SLOTS))
                src, tile = x_t if g.layer == 0 else mid_t[g.layer - 1], g.value(-g.layer * TILES)
                sp.dma_start(x_res[:, g.slot, :], tile_of(src, tile)).then_inc(res_loaded[g.slot], 16)

            def store(g):
                weights_loaded(g)
                sp.wait_ge(out_ready, g.value(1))
                sp.dma_start(tile_of(mid_t[g.layer], g.value(-g.layer * TILES)), x_out[:, g.slot, :])\
                    .then_inc(stored[g.slot], 16)

            def step(i):
                if exists(i + 6):
                    load_inputs(i + 6)
                if exists(i):
                    load_residual(i)
                if exists(i - 3):
                    store(i - 3)

            with nc.allow_non_contiguous_dma(reason="biases and the mask, once"):
                for dst, src in loads:
                    sp.dma_start(dst, src).then_inc(loaded, 16)
            walk_tiles(sp, step, 6, 3)

            def load_group(j):
                weights_loaded(j)
                if due(j.value(-1)):
                    sp.wait_ge(f_z_ready, j.value(-1))
                sp.dma_start(f_in[:, j.par, :, :], group_of(mid_t[2], j.value())).then_inc(f_loaded[j.par], 16)

            def store_group(j):
                weights_loaded(j)
                sp.wait_ge(f_out_ready, j.value(1))
                sp.dma_start(group_of(out_t, j.value()), f_out[:, j.par, :, :]).then_inc(f_stored[j.par], 16)

            def group_step(j):
                if group_exists(j + 2):
                    load_group(j + 2)
                if group_exists(j - 1):
                    store_group(j - 1)

            for s in range(SLOTS):
                sp.wait_ge(stored[s], 16 * G // SLOTS)
            walk_groups(sp, group_step, 2, 1)
            for p in range(2):
                sp.wait_ge(f_stored[p], 16 * GROUPS // 2)

        @block.tensor
        def _(pe):
            def transpose_inputs(g):
                pe.wait_ge(x_loaded[g.slot], g.rounds(-SLOTS))
                if g.layer != SELF:
                    pe.wait_ge(c_loaded[g.slot], g.rounds(-SLOTS + (TILES if g.layer == CROSS else 0)))
                if due(g.value()):
                    pe.wait_ge(in_copied, g.value())
                last = nc.tensor.transpose(in_bank[:, 0:P], x_in[:, g.slot, :], ident[:, :])
                if g.layer != SELF:
                    last = nc.tensor.transpose(in_bank[:, P:2 * P], c_in[:, g.slot, :], ident[:, :])
                last.then_inc(in_transposed, 1)

            def project(g):
                kv = 0 if g.layer == SELF else 1
                pe.wait_ge(in_copied, g.value(1))
                if due(g.value()):
                    pe.wait_ge(v_ready, g.value())
                q_src, kv_src = xcT[:, g.slot, 0, :], xcT[:, g.slot, kv, :]
                nc.tensor.matmul(proj_bank[:, P:2 * P], w_k[:, g.layer, :], kv_src, start=True, stop=True)
                nc.tensor.matmul(proj_bank[:, 0:P], w_q[:, g.layer, :], q_src, start=True, stop=True)
                for b in range(2):
                    for e in range(2):
                        heads = w_v[:, g.layer, :].rearrange("p (c e d) -> p e c d", e=2, d=DH)[:, e, :, :]
                        last = nc.tensor.matmul(proj_bank[e * S:(e + 1) * S, 2 * P + b * S:2 * P + (b + 1) * S],
                                                kv_src[:, b * S:(b + 1) * S], heads, start=True, stop=True)
                last.then_inc(projected, 1)

            def score(g, h):
                pe.wait_ge(q_ready, g.value(1))
                pe.wait_ge(k_spread, g.value(1))
                if due(g.value()):
                    pe.wait_ge(shift_ready[h], g.value())
                for b in range(2):
                    last = nc.tensor.matmul(score_bank[h][b * S:(b + 1) * S, :],
                                            QT[:, g.slot, b * S:(b + 1) * S],
                                            Kx[:, g.par, b, h * HALF:(h + 1) * HALF, :],
                                            start=True, stop=True)
                last.then_inc(scored[h], 1)

            def transpose_probs(g, h):
                pe.wait_ge(exp_ready[h], g.value(1))
                if due(g.value()):
                    pe.wait_ge(pt_copied[h], g.value())
                for c in range(PAIRS):
                    last = nc.tensor.transpose(pt_bank[h][:, c * P:(c + 1) * P],
                                               probs[:, g.par, h, c * P:(c + 1) * P], ident[:, :])
                last.then_inc(probs_transposed[h], 1)

            def weigh_values(g, h):
                pe.wait_ge(pt_copied[h], g.value(1))
                if h == 0:
                    pe.wait_ge(v_ready, g.value(1))
                    if due(g.value()):
                        pe.wait_ge(ot_copied, g.value())
                for b in range(2):
                    for c in range(PAIRS):
                        last = nc.tensor.matmul(
                            ot_bank[32 * c:32 * c + 32, h * P + b * S:h * P + (b + 1) * S],
                            Vx[:, g.slot, b, h * PAIRS + c, :, :],
                            PT[:, g.par, h, c, b * S:(b + 1) * S], start=True, stop=True)
                if h == 1:
                    last.then_inc(pv_done, 1)

            def transpose_back(g):
                pe.wait_ge(ot_copied, g.value(1))
                if due(g.value()):
                    pe.wait_ge(tail_free, g.value())
                for h in range(2):
                    last = nc.tensor.transpose(tail_bank[:, h * P:(h + 1) * P], OT[:, g.par, h, :],
                                               ident[:, :])
                last.then_inc(o_back, 1)

            def transpose_attn(g):
                pe.wait_ge(attn_ready, g.value(1 - TILES))
                nc.tensor.transpose(tail_bank[:, 2 * P:3 * P], attn[:, g.par, :, :], ident[:, :])\
                    .then_inc(attn_transposed, 1)

            def project_out(g):
                pe.wait_ge(attn_copied, g.value(1 - TILES))
                nc.tensor.matmul(tail_bank[:, 3 * P:4 * P], attnT[:, g.par, :], w_o[:, g.layer, :],
                                 start=True, stop=True).then_inc(y_done, 1)

            def step(i):
                if exists(i):
                    transpose_probs(i, 0)
                if exists(i - 1):
                    transpose_back(i - 1)
                if exists(i):
                    transpose_probs(i, 1)
                if exists(i + 1):
                    score(i + 1, 0)
                if exists(i + 3):
                    project(i + 3)
                if exists(i - 1) and (i - 1).layer:
                    transpose_attn(i - 1)
                if exists(i):
                    weigh_values(i, 0)
                if exists(i + 1):
                    score(i + 1, 1)
                if exists(i - 1) and (i - 1).layer:
                    project_out(i - 1)
                if exists(i):
                    weigh_values(i, 1)
                if exists(i + 4):
                    transpose_inputs(i + 4)

            pe.wait_ge(consts_set, 2)
            pe.wait_ge(loaded, LOADED)
            walk_tiles(pe, step, 4, 1)

            hid_bank = score_bank + pt_bank
            y_bank = [ot_bank, tail_bank]

            def transpose_group(j):
                pe.wait_ge(f_loaded[j.par], j.rounds(-2))
                if due(j.value()):
                    pe.wait_ge(f_copied, j.value())
                for t in range(GROUP):
                    last = nc.tensor.transpose(in_bank[:, t * P:(t + 1) * P], f_in[:, j.par, t, :],
                                               ident[:, :])
                last.then_inc(f_transposed, 1)

            def hidden(j):
                pe.wait_ge(f_copied, j.value(1))
                for c in range(FCH):
                    if due(j.value()):
                        pe.wait_ge(hid_ready[c], j.value())
                    nc.tensor.matmul(hid_bank[c][:, :], w_1[:, c * P:(c + 1) * P], f_inT[:, j.par, :],
                                     start=True, stop=True).then_inc(hid_done[c], 1)

            def down(j):
                if due(j.value(-1)):
                    pe.wait_ge(f_y_read, j.value(-1))
                for c in range(FCH):
                    pe.wait_ge(hid_ready[c], j.value(1))
                for t in range(GROUP):
                    for c in range(FCH):
                        last = nc.tensor.matmul(y_bank[j.par][:, t * P:(t + 1) * P],
                                                hidT[:, j.par, c, t * P:(t + 1) * P], w_2[:, c, :],
                                                start=(c == 0), stop=(c == FCH - 1))
                last.then_inc(f_y_done, 1)

            def group_step(j):
                if group_exists(j):
                    hidden(j)
                if group_exists(j + 1):
                    transpose_group(j + 1)
                if group_exists(j):
                    down(j)

            pe.wait_ge(norm_ready, G)
            walk_groups(pe, group_step, 1, 0)

        @block.scalar
        def _(act):
            def copy_inputs(g):
                n = 1 if g.layer == SELF else 2
                act.wait_ge(in_transposed, g.value(1))
                if due(g.value(1 - SLOTS)):
                    act.wait_ge(projected, g.value(1 - SLOTS))
                nc.scalar.activation(xcT[:, g.slot, 0:n, :].rearrange("p n t -> p (n t)"),
                                     in_bank[:, 0:n * P], ACT.Copy).then_inc(in_copied, 1)

            def exponentials(g, h):
                if g.layer == 0:
                    act.wait_ge(mask_set, 1)
                act.wait_ge(shift_ready[h], g.value(1))
                if due(g.value(-1)):
                    act.wait_ge(probs_transposed[h], g.value(-1))
                if g.layer:
                    scale = SCALE
                elif g.r is None:
                    scale = row_scale[:, g.n:g.n + 1]
                else:
                    scale = row_scale[:, bass.ds(g.value(), 1)]
                nc.scalar.activation(probs[:, g.par, h, :],
                                     shifted[:, g.par, h, :, :].rearrange("p h k -> p (h k)"),
                                     ACT.Exp, scale=scale).then_inc(exp_ready[h], 1)

            def copy_pt(g, h):
                act.wait_ge(probs_transposed[h], g.value(1))
                if due(g.value(-1)):
                    act.wait_ge(pv_done, g.value(-1))
                nc.scalar.activation(PT[:, g.par, h, :, :].rearrange("p c q -> p (c q)"),
                                     pt_bank[h][:, :], ACT.Copy).then_inc(pt_copied[h], 1)

            def copy_ot(g):
                act.wait_ge(pv_done, g.value(1))
                if due(g.value(-1)):
                    act.wait_ge(o_back, g.value(-1))
                nc.scalar.activation(OT[:, g.par, :, :].rearrange("p h q -> p (h q)"),
                                     ot_bank[:, 0:2 * P], ACT.Copy).then_inc(ot_copied, 1)

            def copy_attn(g):
                act.wait_ge(attn_transposed, g.value(1 - TILES))
                if due(g.value(-1 - TILES)):
                    act.wait_ge(y_done, g.value(-1 - TILES))
                nc.scalar.activation(attnT[:, g.par, :], tail_bank[:, 2 * P:3 * P], ACT.Copy)\
                    .then_inc(attn_copied, 1)

            def step(i):
                if exists(i):
                    copy_pt(i, 0)
                    copy_pt(i, 1)
                if exists(i - 1) and (i - 1).layer:
                    copy_attn(i - 1)
                if exists(i + 1):
                    exponentials(i + 1, 0)
                if exists(i + 4):
                    copy_inputs(i + 4)
                if exists(i):
                    copy_ot(i)
                if exists(i + 1):
                    exponentials(i + 1, 1)

            walk_tiles(act, step, 4, 1)

            hid_bank = score_bank + pt_bank

            def group_step(j):
                if group_exists(j):
                    for c in range(0, FCH, 2):
                        act.wait_ge(hid_done[c], j.value(1))
                        if due(j.value(-1)):
                            act.wait_ge(f_y_done, j.value(-1))
                        nc.scalar.activation(hidT[:, j.par, c, :], hid_bank[c][:, :], ACT.Relu,
                                             bias=b_1[:, c:c + 1]).then_inc(hid_ready[c], 1)
                if group_exists(j + 1):
                    act.wait_ge(f_transposed, j.value(2))
                    if due(j.value()):
                        act.wait_ge(hid_done[FCH - 1], j.value())
                    nc.scalar.activation(f_inT[:, (j + 1).par, :], in_bank[:, :], ACT.Copy)\
                        .then_inc(f_copied, 1)

            walk_groups(act, group_step, 1, 0)

        @block.vector
        def _(dve):
            def take_projections(g):
                dve.wait_ge(projected, g.value(1))
                if due(g.value(1 - SLOTS)):
                    dve.wait_ge(k_spread, g.value(1 - SLOTS))
                first = g.layer == 0
                nc.vector.tensor_scalar(KT[:, g.slot, :], proj_bank[:, P:2 * P],
                                        b_k[:, g.layer:g.layer + 1], 0.0 if first else None,
                                        ALU.add, ALU.max if first else ALU.bypass).then_inc(k_ready, 1)
                if due(g.value(1 - SLOTS)):
                    dve.wait_ge(scored[1], g.value(1 - SLOTS))
                nc.vector.tensor_scalar(QT[:, g.slot, :], proj_bank[:, 0:P],
                                        b_q[:, g.layer:g.layer + 1], 0.0 if first else None,
                                        ALU.add, ALU.max if first else ALU.bypass).then_inc(q_ready, 1)
                if due(g.value(1 - SLOTS)):
                    dve.wait_ge(pv_done, g.value(1 - SLOTS))
                v_psum = proj_bank[:, 2 * P:3 * P].rearrange("p (b c d) -> p b c d", b=2, d=DH)
                if first:
                    bias = b_v[:, 0, :, :].unsqueeze(1).to_broadcast([P, 2, H // 2, DH])
                    if due(g.value()):
                        dve.wait_ge(v_ready, g.value())
                    nc.vector.tensor_tensor(v_sum[:, :, :, :], v_psum, bias, ALU.add).then_inc(v_added, 1)
                    dve.wait_ge(v_added, g.value(1))
                for e in range(2):
                    rows = slice(e * S, (e + 1) * S)
                    dst = Vx[rows, g.slot, :, :, e, 0:DH]
                    if first:
                        last = nc.vector.tensor_scalar(dst, v_sum[rows, :, :, :], 0.0, None, ALU.max)
                    else:
                        bias = b_v[rows, g.layer, :, :].unsqueeze(1).to_broadcast([S, 2, H // 2, DH])
                        last = nc.vector.tensor_tensor(dst, v_psum[rows, :, :, :], bias, ALU.add)
                last.then_inc(v_ready, 1)

            def maxima(g, h):
                dve.wait_ge(scored[h], g.value(1))
                nc.vector.tensor_reduce(row_max[:, g.par, h * HALF:(h + 1) * HALF],
                                        score_bank[h][:, :].rearrange("p (h k) -> p h k", k=S),
                                        AX.X, ALU.max).then_inc(max_ready[h], 1)

            def shift(g, h):
                dve.wait_ge(max_ready[h], g.value(1))
                if due(g.value(-1)):
                    dve.wait_ge(exp_ready[h], g.value(-1))
                top = row_max[:, g.par, h * HALF:(h + 1) * HALF].unsqueeze(2).to_broadcast([P, HALF, S])
                nc.vector.tensor_tensor(shifted[:, g.par, h, :, :],
                                        score_bank[h][:, :].rearrange("p (h k) -> p h k", k=S),
                                        top, ALU.subtract).then_inc(shift_ready[h], 1)

            def tail_view():
                return tail_bank[:, 0:2 * P].rearrange("p (h c) -> p h c", c=VC)

            def invert(g):
                dve.wait_ge(o_back, g.value(1))
                nc.vector.reciprocal(inv_sum[:, g.par, :], tail_view()[:, :, DH]).then_inc(inv_ready, 1)

            def normalise(g):
                dve.wait_ge(inv_ready, g.value(1))
                inv = inv_sum[:, g.par, :].unsqueeze(2).to_broadcast([P, H, DH])
                if g.layer:
                    if due(g.value(-1 - TILES)):
                        dve.wait_ge(attn_transposed, g.value(-1 - TILES))
                nc.vector.tensor_tensor(attn[:, g.par, :, :], tail_view()[:, :, 0:DH], inv, ALU.mult)\
                    .then_inc(attn_ready if g.layer else tail_free, 1)

            def residual(g):
                dve.wait_ge(res_loaded[g.slot], g.rounds(-SLOTS))
                if due(g.value(1 - SLOTS)):
                    dve.wait_ge(norm_ready, g.value(1 - SLOTS))
                if g.layer == 0:
                    dve.wait_ge(tail_free, g.value(1))
                    nc.vector.tensor_tensor(z[:, g.slot, :], attn[:, g.par, :, :].rearrange("p h d -> p (h d)"),
                                            x_res[:, g.slot, :], ALU.add).then_inc(z_ready, 1)
                else:
                    dve.wait_ge(y_done, g.value(1 - TILES))
                    nc.vector.tensor_tensor(y_x[:, :], tail_bank[:, 3 * P:4 * P], x_res[:, g.slot, :],
                                            ALU.add).then_inc(tail_free, 1)
                    dve.wait_ge(tail_free, g.value(1))
                    nc.vector.tensor_tensor(z[:, g.slot, :], y_x[:, :], b_o[:, g.layer, :],
                                            ALU.add).then_inc(z_ready, 1)

            def moments(g):
                dve.wait_ge(z_ready, g.value(1))
                nc.vector.bn_stats(stats[:, :], z[:, g.slot, :]).then_inc(stats_ready, 1)
                dve.wait_ge(v_ones, 2)
                dve.wait_ge(stats_ready, g.value(1))
                nc.vector.bn_aggr(mean_var[:, g.slot, :], stats[:, :]).then_inc(mean_ready, 1)
                dve.wait_ge(mean_ready, g.value(1))
                nc.vector.tensor_scalar(var_eps[:, g.slot:g.slot + 1], mean_var[:, g.slot, 1:2], EPS, None,
                                        ALU.add).then_inc(var_ready, 1)

            def layer_norm(g):
                dve.wait_ge(rstd_ready, g.value(1))
                if due(g.value(1 - SLOTS)):
                    dve.wait_ge(gamma_done, g.value(1 - SLOTS))
                nc.vector.tensor_scalar(normed[:, g.slot, :], z[:, g.slot, :], mean_var[:, g.slot, 0:1],
                                        rstd[:, g.slot:g.slot + 1], ALU.subtract, ALU.mult)\
                    .then_inc(norm_ready, 1)

            def step(i):
                if exists(i - 1):
                    invert(i - 1)
                if exists(i - 2):
                    layer_norm(i - 2)
                if exists(i - 1):
                    normalise(i - 1)
                if exists(i + 1):
                    maxima(i + 1, 0)
                if exists(i + 3):
                    take_projections(i + 3)
                if exists(i + 1):
                    shift(i + 1, 0)
                if exists(i + 1):
                    maxima(i + 1, 1)
                if exists(i - 1):
                    residual(i - 1)
                if exists(i + 1):
                    shift(i + 1, 1)
                if exists(i - 1):
                    moments(i - 1)

            nc.vector.memset(Vx[:, :, :, :, :, :].rearrange("p s b c e v -> p (s b c e v)"), 0.0)\
                .then_inc(v_zeroed, 1)
            dve.wait_ge(v_zeroed, 1)
            for e in range(2):
                nc.vector.memset(Vx[e * S:(e + 1) * S, :, :, :, e, DH:DH + 1]
                                 .rearrange("p s b c v -> p (s b c v)"), 1.0).then_inc(v_ones, 1)
            dve.wait_ge(loaded, LOADED)
            nc.vector.tensor_copy(mask_f[:, :], mask_i[:, :]).then_inc(mask_cast, 1)
            dve.wait_ge(mask_cast, 1)
            nc.vector.tensor_scalar(row_scale[:, :], mask_f[:, :], 0.0, SCALE, ALU.not_equal, ALU.mult)\
                .then_inc(mask_set, 1)
            dve.wait_ge(v_ones, 2)
            walk_tiles(dve, step, 4, 2)

            hid_bank = score_bank + pt_bank
            y_bank = [ot_bank, tail_bank]

            def hidden(j):
                for c in range(1, FCH, 2):
                    dve.wait_ge(hid_done[c], j.value(1))
                    if due(j.value(-1)):
                        dve.wait_ge(f_y_done, j.value(-1))
                    nc.vector.tensor_scalar(hidT[:, j.par, c, :], hid_bank[c][:, :], b_1[:, c:c + 1], 0.0,
                                            ALU.add, ALU.max).then_inc(hid_ready[c], 1)

            def group_norm(j):
                dve.wait_ge(f_y_done, j.value(1))
                dve.wait_ge(f_loaded[j.par], j.rounds(-2))
                nc.vector.tensor_tensor(f_y[:, :, :],
                                        y_bank[j.par][:, :].rearrange("p (t d) -> p t d", t=GROUP),
                                        f_in[:, j.par, :, :], ALU.add).then_inc(f_y_read, 1)
                dve.wait_ge(f_y_read, j.value(1))
                nc.vector.tensor_tensor(f_z[:, j.par, :, :], f_y[:, :, :],
                                        b_2[:, :].unsqueeze(1).to_broadcast([P, GROUP, D]), ALU.add)\
                    .then_inc(f_z_ready, 1)
                dve.wait_ge(f_z_ready, j.value(1))
                for t in range(GROUP):
                    last = nc.vector.bn_stats(f_stats[:, t, :], f_z[:, j.par, t, :])
                last.then_inc(f_stats_ready, 1)
                dve.wait_ge(v_ones, 2)
                dve.wait_ge(f_stats_ready, j.value(1))
                for t in range(GROUP):
                    last = nc.vector.bn_aggr(f_mv[:, j.par, t, :], f_stats[:, t, :])
                last.then_inc(f_mean_ready, 1)
                dve.wait_ge(f_mean_ready, j.value(1))
                nc.vector.tensor_scalar(f_ve[:, j.par, :], f_mv[:, j.par, :, 1], EPS, None, ALU.add)\
                    .then_inc(f_var_ready, 1)

            def group_finish(j):
                dve.wait_ge(f_rstd_ready, j.value(1))
                if due(j.value(-1)):
                    dve.wait_ge(f_gamma_done, j.value(-1))
                for t in range(GROUP):
                    last = nc.vector.tensor_scalar(f_norm[:, j.par, t, :], f_z[:, j.par, t, :],
                                                   f_mv[:, j.par, t, 0:1], f_rstd[:, j.par, t:t + 1],
                                                   ALU.subtract, ALU.mult)
                last.then_inc(f_norm_ready, 1)

            def group_step(j):
                if group_exists(j):
                    hidden(j)
                if group_exists(j - 1):
                    group_finish(j - 1)
                if group_exists(j):
                    group_norm(j)

            walk_groups(dve, group_step, 0, 1)

        @block.gpsimd
        def _(pool):
            def spread_keys(g):
                pool.wait_ge(k_ready, g.value(1))
                if due(g.value(-1)):
                    pool.wait_ge(scored[1], g.value(-1))
                for b in range(2):
                    keys = KT[:, g.slot, b * S:(b + 1) * S].unsqueeze(1).to_broadcast([P, H, S])
                    only = head_mask[:, :].unsqueeze(2).to_broadcast([P, H, S])
                    last = nc.gpsimd.tensor_tensor(Kx[:, g.par, b, :, :], keys, only, ALU.mult)
                last.then_inc(k_spread, 1)

            def root(g):
                pool.wait_ge(var_ready, g.value(1))
                if due(g.value(1 - SLOTS)):
                    pool.wait_ge(norm_ready, g.value(1 - SLOTS))
                nc.gpsimd.tensor_tensor(rstd[:, g.slot:g.slot + 1], var_eps[:, g.slot:g.slot + 1],
                                        neg_half[:, 0:1], ALU.pow).then_inc(rstd_ready, 1)

            def scale(g):
                pool.wait_ge(norm_ready, g.value(1))
                if due(g.value()):
                    pool.wait_ge(out_ready, g.value())
                nc.gpsimd.tensor_tensor(scaled[:, :], normed[:, g.slot, :], ln_g[:, g.layer, :], ALU.mult)\
                    .then_inc(gamma_done, 1)
                if due(g.rounds()):
                    pool.wait_ge(stored[g.slot], g.rounds())
                pool.wait_ge(gamma_done, g.value(1))
                nc.gpsimd.tensor_tensor(x_out[:, g.slot, :], scaled[:, :], ln_b[:, g.layer, :], ALU.add)\
                    .then_inc(out_ready, 1)

            def step(i):
                if exists(i + 2):
                    spread_keys(i + 2)
                if exists(i - 2):
                    scale(i - 2)
                if exists(i - 1):
                    root(i - 1)

            nc.gpsimd.memset(ident[:, :], 0.0).then_inc(consts_zero, 1)
            nc.gpsimd.memset(head_mask[:, :], 1.0).then_inc(consts_zero, 1)
            nc.gpsimd.memset(neg_half[:, :], -0.5).then_inc(consts_zero, 1)
            pool.wait_ge(consts_zero, 3)
            nc.gpsimd.affine_select(out=ident[:, :], in_=ident[:, :], compare_op=ALU.not_equal, fill=1.0,
                                    base=0, pattern=[[-1, P]], channel_multiplier=1).then_inc(consts_set, 1)
            nc.gpsimd.affine_select(out=head_mask[:, :], in_=head_mask[:, :], compare_op=ALU.is_ge, fill=0.0,
                                    base=0, pattern=[[-DH, H]], channel_multiplier=1).then_inc(consts_band, 1)
            pool.wait_ge(consts_band, 1)
            nc.gpsimd.affine_select(out=head_mask[:, :], in_=head_mask[:, :], compare_op=ALU.is_ge, fill=0.0,
                                    base=DH - 1, pattern=[[DH, H]], channel_multiplier=-1)\
                .then_inc(consts_set, 1)
            pool.wait_ge(consts_set, 2)
            pool.wait_ge(loaded, LOADED)
            walk_tiles(pool, step, 3, 2)

            def group_root(j):
                pool.wait_ge(f_var_ready, j.value(1))
                if due(j.value(-1)):
                    pool.wait_ge(f_norm_ready, j.value(-1))
                nc.gpsimd.tensor_tensor(f_rstd[:, j.par, :], f_ve[:, j.par, :], neg_half[:, :], ALU.pow)\
                    .then_inc(f_rstd_ready, 1)

            def group_scale(j):
                pool.wait_ge(f_norm_ready, j.value(1))
                if due(j.value()):
                    pool.wait_ge(f_out_ready, j.value())
                gamma = ln_g[:, LAYERS, :].unsqueeze(1).to_broadcast([P, GROUP, D])
                beta = ln_b[:, LAYERS, :].unsqueeze(1).to_broadcast([P, GROUP, D])
                nc.gpsimd.tensor_tensor(f_scaled[:, :, :], f_norm[:, j.par, :, :], gamma, ALU.mult)\
                    .then_inc(f_gamma_done, 1)
                pool.wait_ge(f_gamma_done, j.value(1))
                if due(j.rounds()):
                    pool.wait_ge(f_stored[j.par], j.rounds())
                nc.gpsimd.tensor_tensor(f_out[:, j.par, :, :], f_scaled[:, :, :], beta, ALU.add)\
                    .then_inc(f_out_ready, 1)

            def group_step(j):
                if group_exists(j):
                    group_root(j)
                if group_exists(j - 1):
                    group_scale(j - 1)

            walk_groups(pool, group_step, 0, 1)


def kernel(**inputs):
    import concourse.bacc as bacc
    from concourse.bass_utils import run_bass_kernel_spmd

    nc = bacc.Bacc("TRN2", target_bir_lowering=False, num_devices=1)
    arrays, args = {}, {}
    for name, value in inputs.items():
        v = np.ascontiguousarray(value)
        if v.ndim == 3:
            v = v.reshape(B * S, D)
        arrays[name] = v
        args[name] = nc.dram_tensor(name, v.shape, mybir.dt.from_np(v.dtype), kind="ExternalInput").ap()
    out = nc.dram_tensor("out", (B * S, D), F32, kind="ExternalOutput").ap()
    mid = [nc.dram_tensor(f"layer{n}_out", (B * S, D), F32, kind="Internal").ap() for n in range(LAYERS)]
    build(nc, args, out, mid)
    got = run_bass_kernel_spmd(nc, [arrays], core_ids=[0])
    return got.results[0]["out"].reshape(B, S, D)
```

```python
from contextlib import ExitStack

import numpy as np

import concourse.bass as bass
from concourse import mybir

F32 = mybir.dt.float32
ALU = mybir.AluOpType
ACT = mybir.ActivationFunctionType
AX = mybir.AxisListType

B, S, D, H, FF = 128, 64, 128, 16, 512
DH = D // H
P = 128
TILES = B * S // P
LAYERS = 3
G = LAYERS * TILES
HALF = H // 2
PAIRS = HALF // 2
VC = 2 * DH
EPS = 1e-5
SCALE = float(1.0 / np.sqrt(np.float32(DH)))
SLOTS = 4
FCH = FF // P
GROUP = 4
GROUPS = TILES // GROUP
SELF, CROSS = 1, 2


class At:

    def __init__(self, n, stride, r=None):
        self.n, self.stride, self.r = n, stride, r

    def __add__(self, k):
        return At(self.n + k, self.stride, self.r)

    def __sub__(self, k):
        return At(self.n - k, self.stride, self.r)

    def value(self, k=0):
        return self.n + k if self.r is None else self.r * self.stride + (self.n + k)

    def rounds(self, k=0):
        n = (self.n - k) // self.stride
        return 16 * n if self.r is None else self.r * 16 + 16 * n

    @property
    def layer(self):
        return self.n // TILES

    @property
    def slot(self):
        return self.n % SLOTS

    @property
    def par(self):
        return self.n % 2


def due(count):
    return not isinstance(count, int) or count >= 1


def walk_tiles(eng, step, before, after):
    for n in range(-before, 2 * SLOTS):
        step(At(n, SLOTS))
    for layer in range(LAYERS):
        first, last = layer * TILES + 2 * SLOTS, (layer + 1) * TILES - 2 * SLOTS
        with eng.Fori(0, (last - first) // SLOTS) as r:
            for k in range(SLOTS):
                step(At(first + k, SLOTS, r))
        end = G + after if layer == LAYERS - 1 else (layer + 1) * TILES + 2 * SLOTS
        for n in range(last, end):
            step(At(n, SLOTS))


def walk_groups(eng, step, before, after):
    for n in range(-before, 4):
        step(At(n, 2))
    with eng.Fori(0, (GROUPS - 8) // 2) as r:
        for k in range(2):
            step(At(4 + k, 2, r))
    for n in range(GROUPS - 4, GROUPS + after):
        step(At(n, 2))


def exists(g):
    return 0 <= g.n < G


def group_exists(j):
    return 0 <= j.n < GROUPS


def build(nc, a, out, mid):
    ctx = ExitStack()
    with ctx:
        def sb(name, shape, dt=F32):
            return ctx.enter_context(nc.sbuf_tensor(name, shape, dt))

        def bank(name):
            return ctx.enter_context(nc.psum_tensor(name, [P, 512], F32))

        def sem(name):
            return ctx.enter_context(nc.semaphore(name))

        ident = sb("ident", [P, P])
        head_mask = sb("head_mask", [P, 2, HALF])
        own_head = sb("own_head", [P, HALF])
        neg_half = sb("neg_half", [P, GROUP])
        w_q = sb("w_q", [P, LAYERS, D])
        w_k = sb("w_k", [P, LAYERS, D])
        w_v = sb("w_v", [P, LAYERS, D])
        w_o = sb("w_o", [P, LAYERS, D])
        b_q = sb("b_q", [P, LAYERS])
        b_k = sb("b_k", [P, LAYERS])
        b_v = sb("b_v", [1, LAYERS, D])
        ones_row = sb("ones_row", [1, S])
        b_o = sb("b_o", [P, LAYERS, D])
        ln_g = sb("ln_g", [P, LAYERS + 1, D])
        ln_b = sb("ln_b", [P, LAYERS + 1, D])
        w_1 = sb("w_1", [P, FF])
        b_1 = sb("b_1", [P, FCH])
        w_2 = sb("w_2", [P, FCH, D])
        b_2 = sb("b_2", [P, D])
        mask_i = sb("mask_i", [P, TILES], mybir.dt.int32)
        mask_f = sb("mask_f", [P, TILES])
        row_scale = sb("row_scale", [P, TILES])

        x_in = sb("x_in", [P, SLOTS, D])
        c_in = sb("c_in", [P, SLOTS, D])
        x_res = sb("x_res", [P, SLOTS, D])
        xcT = sb("xcT", [P, SLOTS, 2, P])
        QT = sb("QT", [P, SLOTS, 2, P])
        KT = sb("KT", [P, SLOTS, P])
        Kx = sb("Kx", [P, 2, 2, HALF, S])
        Vx = sb("Vx", [P, SLOTS, 2, H // 2, 2, VC])
        row_max = sb("row_max", [P, 2, H])
        shifted = sb("shifted", [P, 2, 2, HALF, S])
        probs = sb("probs", [P, 2, 2, HALF * S])
        PT = sb("PT", [P, 2, 2, PAIRS, P])
        OT = sb("OT", [P, 2, 2, P])
        inv_sum = sb("inv_sum", [P, 2, H])
        attn = sb("attn", [P, 2, H, DH])
        attnT = sb("attnT", [P, 2, P])
        x_bias = sb("x_bias", [P, SLOTS, D])
        z = sb("z", [P, SLOTS, D])
        stats = sb("stats", [P, 6])
        mean_var = sb("mean_var", [P, SLOTS, 2])
        var_eps = sb("var_eps", [P, SLOTS])
        rstd = sb("rstd", [P, SLOTS])
        normed = sb("normed", [P, SLOTS, D])
        scaled = sb("scaled", [P, D])
        x_out = sb("x_out", [P, SLOTS, D])

        f_in = sb("f_in", [P, 2, GROUP, D])
        f_inT = sb("f_inT", [P, 2, GROUP * P])
        hidT = sb("hidT", [P, 2, FCH, GROUP * P])
        f_y = sb("f_y", [P, GROUP, D])
        f_z = sb("f_z", [P, 2, GROUP, D])
        f_stats = sb("f_stats", [P, GROUP, 6])
        f_mv = sb("f_mv", [P, 2, GROUP, 2])
        f_ve = sb("f_ve", [P, 2, GROUP])
        f_rstd = sb("f_rstd", [P, 2, GROUP])
        f_norm = sb("f_norm", [P, 2, GROUP, D])
        f_scaled = sb("f_scaled", [P, GROUP, D])
        f_out = sb("f_out", [P, 2, GROUP, D])

        in_bank = bank("in_bank")
        proj_bank = bank("proj_bank")
        score_bank = [bank("score_bank0"), bank("score_bank1")]
        pt_bank = [bank("pt_bank0"), bank("pt_bank1")]
        ot_bank = bank("ot_bank")
        tail_bank = bank("tail_bank")

        loaded = sem("loaded")
        loaded_late = sem("loaded_late")
        consts_zero = sem("consts_zero")
        consts_band = sem("consts_band")
        consts_set = sem("consts_set")
        mask_cast = sem("mask_cast")
        mask_set = sem("mask_set")
        q_zeroed = sem("q_zeroed")
        v_zeroed = sem("v_zeroed")
        v_ones = sem("v_ones")
        x_loaded = [sem(f"x_loaded{s}") for s in range(SLOTS)]
        c_loaded = [sem(f"c_loaded{s}") for s in range(SLOTS)]
        res_loaded = [sem(f"res_loaded{s}") for s in range(SLOTS)]
        stored = [sem(f"stored{s}") for s in range(SLOTS)]
        in_transposed = sem("in_transposed")
        in_copied = sem("in_copied")
        projected = sem("projected")
        k_ready = sem("k_ready")
        q_ready = sem("q_ready")
        v_ready = sem("v_ready")
        k_spread = sem("k_spread")
        scored = [sem("scored0"), sem("scored1")]
        max_ready = [sem("max_ready0"), sem("max_ready1")]
        shift_ready = [sem("shift_ready0"), sem("shift_ready1")]
        exp_ready = [sem("exp_ready0"), sem("exp_ready1")]
        probs_transposed = [sem("probs_transposed0"), sem("probs_transposed1")]
        pt_copied = [sem("pt_copied0"), sem("pt_copied1")]
        pv_done = sem("pv_done")
        ot_copied = sem("ot_copied")
        o_back = sem("o_back")
        inv_ready = sem("inv_ready")
        attn_ready = sem("attn_ready")
        attn_transposed = sem("attn_transposed")
        attn_copied = sem("attn_copied")
        y_done = sem("y_done")
        tail_free = sem("tail_free")
        res_biased = sem("res_biased")
        z_ready = sem("z_ready")
        stats_ready = sem("stats_ready")
        mean_ready = sem("mean_ready")
        var_ready = sem("var_ready")
        rstd_ready = sem("rstd_ready")
        norm_ready = sem("norm_ready")
        gamma_done = sem("gamma_done")
        out_ready = sem("out_ready")
        f_loaded = [sem("f_loaded0"), sem("f_loaded1")]
        f_stored = [sem("f_stored0"), sem("f_stored1")]
        f_transposed = sem("f_transposed")
        f_copied = sem("f_copied")
        hid_done = [sem(f"hid_done{c}") for c in range(FCH)]
        hid_ready = [sem(f"hid_ready{c}") for c in range(FCH)]
        f_y_done = sem("f_y_done")
        f_y_read = sem("f_y_read")
        f_z_ready = sem("f_z_ready")
        f_stats_ready = sem("f_stats_ready")
        f_mean_ready = sem("f_mean_ready")
        f_var_ready = sem("f_var_ready")
        f_rstd_ready = sem("f_rstd_ready")
        f_norm_ready = sem("f_norm_ready")
        f_gamma_done = sem("f_gamma_done")
        f_out_ready = sem("f_out_ready")

        block = ctx.enter_context(nc.Block())

        def tiles_of(t):
            return t.rearrange("(t p) d -> t p d", p=P)

        x_t, c_t, out_t = tiles_of(a["x"]), tiles_of(a["ctx_1024"]), tiles_of(out)
        mid_t = [tiles_of(m) for m in mid]

        def tile_of(t, i):
            return t[i, :, :] if isinstance(i, int) else t[bass.ds(i, 1), :, :].rearrange("t p d -> (t p) d")

        def group_of(t, i):
            v = t.rearrange("(j t) p d -> j p t d", t=GROUP)
            return v[i] if isinstance(i, int) else v[bass.ds(i, 1)].rearrange("j p t d -> (j p) t d")

        def column(v, n):
            return v.rearrange("(c p) -> p c", p=n)

        def row(v):
            return v.rearrange("(a n) -> a n", a=1).to_broadcast([P, v.shape[0]])

        L1 = "L1_xattn_"
        kinds = ["L0_xattn_W", L1 + "sa_w", L1 + "ca_w"]
        biases = ["L0_xattn_b", L1 + "sa_b", L1 + "ca_b"]
        first_layer, late = [], [(mask_i[:, :], a["mask_BxS2_ik0"].rearrange("(t b) s -> (b s) t", b=P // S))]
        for n in range(LAYERS):
            loads = late if n else first_layer
            loads += [(w_k[:, n, :], a[kinds[n] + "k"]), (w_q[:, n, :], a[kinds[n] + "q"]),
                      (w_v[:, n, :], a[kinds[n] + "v"]),
                      (b_k[:, n:n + 1], column(a[biases[n] + "k"], P)),
                      (b_q[:, n:n + 1], column(a[biases[n] + "q"], P)),
                      (b_v[:, n, :], a[biases[n] + "v"].rearrange("(a n) -> a n", a=1))]
            if n:
                loads += [(w_o[:, n, :], a[kinds[n] + "o"]), (b_o[:, n, :], row(a[biases[n] + "o"]))]
        for n, (g, b) in enumerate([("L0_xattn_gamma", "L0_xattn_beta")] +
                                   [(L1 + f"ln{i}_g", L1 + f"ln{i}_b") for i in (1, 2, 3)]):
            late += [(ln_g[:, n, :], row(a[g])), (ln_b[:, n, :], row(a[b]))]
        late += [(w_1[:, :], a[L1 + "ff_w1"]), (b_1[:, :], column(a[L1 + "ff_b1"], P)),
                 (w_2[:, :, :], a[L1 + "ff_w2"].rearrange("(c p) n -> p c n", p=P)),
                 (b_2[:, :], row(a[L1 + "ff_b2"]))]
        LOADED, LOADED_LATE = 16 * len(first_layer), 16 * len(late)

        @block.sync
        def _(sp):
            def weights_loaded(g):
                if g.r is not None:
                    sp.wait_ge(loaded, LOADED)

            def load_inputs(g):
                weights_loaded(g)
                if due(g.value(1 - SLOTS)):
                    sp.wait_ge(in_transposed, g.value(1 - SLOTS))
                src, tile = x_t if g.layer == 0 else mid_t[g.layer - 1], g.value(-g.layer * TILES)
                sp.dma_start(x_in[:, g.slot, :], tile_of(src, tile)).then_inc(x_loaded[g.slot], 16)
                if g.layer != SELF:
                    sp.dma_start(c_in[:, g.slot, :], tile_of(c_t, tile)).then_inc(c_loaded[g.slot], 16)

            def load_residual(g):
                weights_loaded(g)
                if due(g.value(1 - SLOTS)):
                    sp.wait_ge(z_ready, g.value(1 - SLOTS))
                src, tile = x_t if g.layer == 0 else mid_t[g.layer - 1], g.value(-g.layer * TILES)
                sp.dma_start(x_res[:, g.slot, :], tile_of(src, tile)).then_inc(res_loaded[g.slot], 16)

            def store(g):
                weights_loaded(g)
                sp.wait_ge(out_ready, g.value(1))
                sp.dma_start(tile_of(mid_t[g.layer], g.value(-g.layer * TILES)), x_out[:, g.slot, :])\
                    .then_inc(stored[g.slot], 16)

            def step(i):
                if exists(i + 6):
                    load_inputs(i + 6)
                if exists(i + 1):
                    load_residual(i + 1)
                if exists(i - 3):
                    store(i - 3)

            with nc.allow_non_contiguous_dma(reason="biases and the mask, once"):
                load_inputs(At(0, SLOTS))
                for dst, src in first_layer:
                    sp.dma_start(dst, src).then_inc(loaded, 16)
            walk_tiles(sp, step, 5, 3)

            def load_group(j):
                weights_loaded(j)
                if due(j.value(-1)):
                    sp.wait_ge(f_z_ready, j.value(-1))
                sp.dma_start(f_in[:, j.par, :, :], group_of(mid_t[2], j.value())).then_inc(f_loaded[j.par], 16)

            def store_group(j):
                weights_loaded(j)
                sp.wait_ge(f_out_ready, j.value(1))
                sp.dma_start(group_of(out_t, j.value()), f_out[:, j.par, :, :]).then_inc(f_stored[j.par], 16)

            def group_step(j):
                if group_exists(j + 2):
                    load_group(j + 2)
                if group_exists(j - 1):
                    store_group(j - 1)

            for s in range(SLOTS):
                sp.wait_ge(stored[s], 16 * G // SLOTS)
            walk_groups(sp, group_step, 2, 1)
            for p in range(2):
                sp.wait_ge(f_stored[p], 16 * GROUPS // 2)

        @block.tensor
        def _(pe):
            def transpose_inputs(g):
                pe.wait_ge(x_loaded[g.slot], g.rounds(-SLOTS))
                if g.layer != SELF:
                    pe.wait_ge(c_loaded[g.slot], g.rounds(-SLOTS + (TILES if g.layer == CROSS else 0)))
                if due(g.value()):
                    pe.wait_ge(in_copied, g.value())
                last = nc.tensor.transpose(in_bank[:, 0:P], x_in[:, g.slot, :], ident[:, :])
                if g.layer != SELF:
                    last = nc.tensor.transpose(in_bank[:, P:2 * P], c_in[:, g.slot, :], ident[:, :])
                last.then_inc(in_transposed, 1)

            def project(g):
                if g.n == TILES:
                    pe.wait_ge(loaded_late, LOADED_LATE)
                kv = 0 if g.layer == SELF else 1
                pe.wait_ge(in_copied, g.value(1))
                if due(g.value()):
                    pe.wait_ge(v_ready, g.value())
                q_src, kv_src = xcT[:, g.slot, 0, :], xcT[:, g.slot, kv, :]
                nc.tensor.matmul(proj_bank[:, P:2 * P], w_k[:, g.layer, :], kv_src, start=True, stop=True)
                nc.tensor.matmul(proj_bank[:, 0:P], w_q[:, g.layer, :], q_src, start=True, stop=True)
                for e in range(2):
                    bias = b_v[:, g.layer, :].rearrange("p (c e d) -> p e c d", e=2, d=DH)[:, e, :, :]
                    nc.tensor.matmul(proj_bank[e * S:(e + 1) * S, 2 * P:3 * P], ones_row[:, :],
                                     bias.unsqueeze(1).to_broadcast([1, 2, H // 2, DH]),
                                     start=True, stop=False, skip_group_check=True)
                for b in range(2):
                    for e in range(2):
                        heads = w_v[:, g.layer, :].rearrange("p (c e d) -> p e c d", e=2, d=DH)[:, e, :, :]
                        last = nc.tensor.matmul(proj_bank[e * S:(e + 1) * S, 2 * P + b * S:2 * P + (b + 1) * S],
                                                kv_src[:, b * S:(b + 1) * S], heads, start=False,
                                                stop=True, skip_group_check=True)
                last.then_inc(projected, 1)

            def score(g, h):
                pe.wait_ge(q_ready, g.value(1))
                pe.wait_ge(k_spread, g.value(1))
                if due(g.value()):
                    pe.wait_ge(shift_ready[h], g.value())
                for b in range(2):
                    last = nc.tensor.matmul(score_bank[h][b * S:(b + 1) * S, :],
                                            QT[:, g.slot, h, b * S:(b + 1) * S],
                                            Kx[:, g.par, b, :, :],
                                            start=True, stop=True)
                last.then_inc(scored[h], 1)

            def transpose_probs(g, h):
                pe.wait_ge(exp_ready[h], g.value(1))
                if due(g.value()):
                    pe.wait_ge(pt_copied[h], g.value())
                for c in range(PAIRS):
                    last = nc.tensor.transpose(pt_bank[h][:, c * P:(c + 1) * P],
                                               probs[:, g.par, h, c * P:(c + 1) * P], ident[:, :])
                last.then_inc(probs_transposed[h], 1)

            def weigh_values(g, h):
                pe.wait_ge(pt_copied[h], g.value(1))
                if h == 0:
                    pe.wait_ge(v_ready, g.value(1))
                    if due(g.value()):
                        pe.wait_ge(ot_copied, g.value())
                for b in range(2):
                    for c in range(PAIRS):
                        last = nc.tensor.matmul(
                            ot_bank[32 * c:32 * c + 32, h * P + b * S:h * P + (b + 1) * S],
                            Vx[:, g.slot, b, h * PAIRS + c, :, :],
                            PT[:, g.par, h, c, b * S:(b + 1) * S], start=True, stop=True)
                if h == 1:
                    last.then_inc(pv_done, 1)

            def transpose_back(g):
                pe.wait_ge(ot_copied, g.value(1))
                if (g - 1).layer == 0 and due(g.value()):
                    pe.wait_ge(tail_free, g.value())
                elif due(g.value()):
                    pe.wait_ge(z_ready, g.value())
                for h in range(2):
                    last = nc.tensor.transpose(tail_bank[:, h * P:(h + 1) * P], OT[:, g.par, h, :],
                                               ident[:, :])
                last.then_inc(o_back, 1)

            def transpose_attn(g):
                pe.wait_ge(attn_ready, g.value(1 - TILES))
                nc.tensor.transpose(tail_bank[:, 2 * P:3 * P], attn[:, g.par, :, :], ident[:, :])\
                    .then_inc(attn_transposed, 1)

            def project_out(g):
                if g.n == TILES:
                    pe.wait_ge(loaded_late, LOADED_LATE)
                pe.wait_ge(attn_copied, g.value(1 - TILES))
                nc.tensor.matmul(tail_bank[:, 3 * P:4 * P], attnT[:, g.par, :], w_o[:, g.layer, :],
                                 start=True, stop=True).then_inc(y_done, 1)

            def step(i):
                if exists(i + 1):
                    score(i + 1, 0)
                if exists(i):
                    transpose_probs(i, 0)
                if exists(i - 1):
                    transpose_back(i - 1)
                if exists(i + 1):
                    score(i + 1, 1)
                if exists(i):
                    transpose_probs(i, 1)
                if exists(i + 3):
                    project(i + 3)
                if exists(i - 1) and (i - 1).layer:
                    transpose_attn(i - 1)
                if exists(i):
                    weigh_values(i, 0)
                if exists(i + 4):
                    transpose_inputs(i + 4)
                if exists(i - 1) and (i - 1).layer:
                    project_out(i - 1)
                if exists(i):
                    weigh_values(i, 1)

            pe.wait_ge(consts_set, 2)
            pe.wait_ge(loaded, LOADED)
            walk_tiles(pe, step, 4, 1)

            hid_bank = score_bank + pt_bank
            y_bank = [ot_bank, tail_bank]

            def transpose_group(j):
                pe.wait_ge(f_loaded[j.par], j.rounds(-2))
                if due(j.value()):
                    pe.wait_ge(f_copied, j.value())
                for t in range(GROUP):
                    last = nc.tensor.transpose(in_bank[:, t * P:(t + 1) * P], f_in[:, j.par, t, :],
                                               ident[:, :])
                last.then_inc(f_transposed, 1)

            def hidden(j):
                pe.wait_ge(f_copied, j.value(1))
                for c in range(FCH):
                    if due(j.value()):
                        pe.wait_ge(hid_ready[c], j.value())
                    nc.tensor.matmul(hid_bank[c][:, :], w_1[:, c * P:(c + 1) * P], f_inT[:, j.par, :],
                                     start=True, stop=True).then_inc(hid_done[c], 1)

            def down(j):
                if due(j.value(-1)):
                    pe.wait_ge(f_y_read, j.value(-1))
                for c in range(FCH):
                    pe.wait_ge(hid_ready[c], j.value(1))
                for t in range(GROUP):
                    for c in range(FCH):
                        last = nc.tensor.matmul(y_bank[j.par][:, t * P:(t + 1) * P],
                                                hidT[:, j.par, c, t * P:(t + 1) * P], w_2[:, c, :],
                                                start=(c == 0), stop=(c == FCH - 1))
                last.then_inc(f_y_done, 1)

            def group_step(j):
                if group_exists(j):
                    hidden(j)
                if group_exists(j + 1):
                    transpose_group(j + 1)
                if group_exists(j):
                    down(j)

            pe.wait_ge(norm_ready, G)
            pe.wait_ge(loaded_late, LOADED_LATE)
            walk_groups(pe, group_step, 1, 0)

        @block.scalar
        def _(act):
            def copy_inputs(g):
                n = 1 if g.layer == SELF else 2
                act.wait_ge(in_transposed, g.value(1))
                if due(g.value(1 - SLOTS)):
                    act.wait_ge(projected, g.value(1 - SLOTS))
                nc.scalar.activation(xcT[:, g.slot, 0:n, :].rearrange("p n t -> p (n t)"),
                                     in_bank[:, 0:n * P], ACT.Copy).then_inc(in_copied, 1)

            def exponentials(g, h):
                if g.layer == 0:
                    act.wait_ge(mask_set, 1)
                act.wait_ge(shift_ready[h], g.value(1))
                if due(g.value(-1)):
                    act.wait_ge(probs_transposed[h], g.value(-1))
                if g.layer:
                    scale = SCALE
                elif g.r is None:
                    scale = row_scale[:, g.n:g.n + 1]
                else:
                    scale = row_scale[:, bass.ds(g.value(), 1)]
                nc.scalar.activation(probs[:, g.par, h, :],
                                     shifted[:, g.par, h, :, :].rearrange("p h k -> p (h k)"),
                                     ACT.Exp, scale=scale).then_inc(exp_ready[h], 1)

            def take_projections(g):
                if g.n == TILES:
                    act.wait_ge(loaded_late, LOADED_LATE)
                func = ACT.Relu if g.layer == 0 else ACT.Identity
                act.wait_ge(projected, g.value(1))
                if due(g.value(1 - SLOTS)):
                    act.wait_ge(k_spread, g.value(1 - SLOTS))
                nc.scalar.activation(KT[:, g.slot, :], proj_bank[:, P:2 * P], func,
                                     bias=b_k[:, g.layer:g.layer + 1]).then_inc(k_ready, 1)
                if due(g.value(1 - SLOTS)):
                    act.wait_ge(scored[1], g.value(1 - SLOTS))
                for h in range(2):
                    rows = slice(h * HALF * DH, (h + 1) * HALF * DH)
                    last = nc.scalar.activation(QT[rows, g.slot, h, :], proj_bank[rows, 0:P], func,
                                                bias=b_q[rows, g.layer:g.layer + 1])
                last.then_inc(q_ready, 1)
                if due(g.value(1 - SLOTS)):
                    act.wait_ge(pv_done, g.value(1 - SLOTS))
                for e in range(2):
                    rows = slice(e * S, (e + 1) * S)
                    last = nc.scalar.activation(
                        Vx[rows, g.slot, :, :, e, 0:DH],
                        proj_bank[rows, 2 * P:3 * P].rearrange("p (b c d) -> p b c d", b=2, d=DH), func)
                last.then_inc(v_ready, 1)

            def copy_pt(g, h):
                act.wait_ge(probs_transposed[h], g.value(1))
                if due(g.value(-1)):
                    act.wait_ge(pv_done, g.value(-1))
                nc.scalar.activation(PT[:, g.par, h, :, :].rearrange("p c q -> p (c q)"),
                                     pt_bank[h][:, :], ACT.Copy).then_inc(pt_copied[h], 1)

            def copy_ot(g):
                act.wait_ge(pv_done, g.value(1))
                if due(g.value(-1)):
                    act.wait_ge(o_back, g.value(-1))
                nc.scalar.activation(OT[:, g.par, :, :].rearrange("p h q -> p (h q)"),
                                     ot_bank[:, 0:2 * P], ACT.Copy).then_inc(ot_copied, 1)

            def copy_attn(g):
                act.wait_ge(attn_transposed, g.value(1 - TILES))
                if due(g.value(-1 - TILES)):
                    act.wait_ge(y_done, g.value(-1 - TILES))
                nc.scalar.activation(attnT[:, g.par, :], tail_bank[:, 2 * P:3 * P], ACT.Copy)\
                    .then_inc(attn_copied, 1)

            def step(i):
                if exists(i):
                    copy_pt(i, 0)
                if exists(i + 1):
                    exponentials(i + 1, 0)
                if exists(i):
                    copy_pt(i, 1)
                if exists(i - 1) and (i - 1).layer:
                    copy_attn(i - 1)
                if exists(i + 3):
                    take_projections(i + 3)
                if exists(i + 4):
                    copy_inputs(i + 4)
                if exists(i + 1):
                    exponentials(i + 1, 1)
                if exists(i):
                    copy_ot(i)

            with nc.allow_non_contiguous_dma(reason="biases and the mask, once"):
                for dst, src in late:
                    act.dma_start(dst, src).then_inc(loaded_late, 16)
            act.wait_ge(loaded, LOADED)
            act.wait_ge(q_zeroed, 1)
            act.wait_ge(v_ones, 2)
            walk_tiles(act, step, 4, 1)

            hid_bank = score_bank + pt_bank

            def group_step(j):
                if group_exists(j):
                    for c in range(0, FCH, 2):
                        act.wait_ge(hid_done[c], j.value(1))
                        if due(j.value(-1)):
                            act.wait_ge(f_y_done, j.value(-1))
                        nc.scalar.activation(hidT[:, j.par, c, :], hid_bank[c][:, :], ACT.Relu,
                                             bias=b_1[:, c:c + 1]).then_inc(hid_ready[c], 1)
                if group_exists(j + 1):
                    act.wait_ge(f_transposed, j.value(2))
                    if due(j.value()):
                        act.wait_ge(hid_done[FCH - 1], j.value())
                    nc.scalar.activation(f_inT[:, (j + 1).par, :], in_bank[:, :], ACT.Copy)\
                        .then_inc(f_copied, 1)

            walk_groups(act, group_step, 1, 0)

        @block.vector
        def _(dve):
            def maxima(g, h):
                dve.wait_ge(scored[h], g.value(1))
                nc.vector.tensor_reduce(row_max[:, g.par, h * HALF:(h + 1) * HALF],
                                        score_bank[h][:, :].rearrange("p (h k) -> p h k", k=S),
                                        AX.X, ALU.max).then_inc(max_ready[h], 1)

            def shift(g, h):
                dve.wait_ge(max_ready[h], g.value(1))
                if due(g.value(-1)):
                    dve.wait_ge(exp_ready[h], g.value(-1))
                top = row_max[:, g.par, h * HALF:(h + 1) * HALF].unsqueeze(2).to_broadcast([P, HALF, S])
                nc.vector.tensor_tensor(shifted[:, g.par, h, :, :],
                                        score_bank[h][:, :].rearrange("p (h k) -> p h k", k=S),
                                        top, ALU.subtract).then_inc(shift_ready[h], 1)

            def tail_view():
                return tail_bank[:, 0:2 * P].rearrange("p (h c) -> p h c", c=VC)

            def invert(g):
                dve.wait_ge(o_back, g.value(1))
                nc.vector.reciprocal(inv_sum[:, g.par, :], tail_view()[:, :, DH]).then_inc(inv_ready, 1)

            def normalise(g):
                dve.wait_ge(inv_ready, g.value(1))
                inv = inv_sum[:, g.par, :].unsqueeze(2).to_broadcast([P, H, DH])
                if g.layer:
                    if due(g.value(-1 - TILES)):
                        dve.wait_ge(attn_transposed, g.value(-1 - TILES))
                nc.vector.tensor_tensor(attn[:, g.par, :, :], tail_view()[:, :, 0:DH], inv, ALU.mult)\
                    .then_inc(attn_ready if g.layer else tail_free, 1)

            def residual(g):
                if due(g.value(1 - SLOTS)):
                    dve.wait_ge(norm_ready, g.value(1 - SLOTS))
                if g.layer == 0:
                    dve.wait_ge(res_loaded[g.slot], g.rounds(-SLOTS))
                    dve.wait_ge(tail_free, g.value(1))
                    nc.vector.tensor_tensor(z[:, g.slot, :], attn[:, g.par, :, :].rearrange("p h d -> p (h d)"),
                                            x_res[:, g.slot, :], ALU.add).then_inc(z_ready, 1)
                else:
                    dve.wait_ge(y_done, g.value(1 - TILES))
                    dve.wait_ge(res_biased, g.value(1 - TILES))
                    nc.vector.tensor_tensor(z[:, g.slot, :], tail_bank[:, 3 * P:4 * P], x_bias[:, g.slot, :],
                                            ALU.add).then_inc(z_ready, 1)

            def moments(g):
                dve.wait_ge(z_ready, g.value(1))
                nc.vector.bn_stats(stats[:, :], z[:, g.slot, :]).then_inc(stats_ready, 1)
                dve.wait_ge(v_ones, 2)
                dve.wait_ge(stats_ready, g.value(1))
                nc.vector.bn_aggr(mean_var[:, g.slot, :], stats[:, :]).then_inc(mean_ready, 1)
                dve.wait_ge(mean_ready, g.value(1))
                nc.vector.tensor_scalar(var_eps[:, g.slot:g.slot + 1], mean_var[:, g.slot, 1:2], EPS, None,
                                        ALU.add).then_inc(var_ready, 1)

            def layer_norm(g):
                dve.wait_ge(rstd_ready, g.value(1))
                if due(g.value(1 - SLOTS)):
                    dve.wait_ge(gamma_done, g.value(1 - SLOTS))
                nc.vector.tensor_scalar(normed[:, g.slot, :], z[:, g.slot, :], mean_var[:, g.slot, 0:1],
                                        rstd[:, g.slot:g.slot + 1], ALU.subtract, ALU.mult)\
                    .then_inc(norm_ready, 1)

            def step(i):
                if exists(i + 1):
                    maxima(i + 1, 0)
                if exists(i - 1):
                    invert(i - 1)
                if exists(i + 1):
                    shift(i + 1, 0)
                if exists(i - 1):
                    normalise(i - 1)
                if exists(i - 2):
                    layer_norm(i - 2)
                if exists(i + 1):
                    maxima(i + 1, 1)
                if exists(i + 1):
                    shift(i + 1, 1)
                if exists(i - 1):
                    residual(i - 1)
                if exists(i - 1):
                    moments(i - 1)

            nc.vector.memset(Vx[:, :, :, :, :, :].rearrange("p s b c e v -> p (s b c e v)"), 0.0)\
                .then_inc(v_zeroed, 1)
            nc.vector.memset(QT[:, :, :, :].rearrange("p s h t -> p (s h t)"), 0.0).then_inc(q_zeroed, 1)
            dve.wait_ge(v_zeroed, 1)
            for e in range(2):
                nc.vector.memset(Vx[e * S:(e + 1) * S, :, :, :, e, DH:DH + 1]
                                 .rearrange("p s b c v -> p (s b c v)"), 1.0).then_inc(v_ones, 1)
            dve.wait_ge(loaded_late, LOADED_LATE)
            nc.vector.tensor_copy(mask_f[:, :], mask_i[:, :]).then_inc(mask_cast, 1)
            dve.wait_ge(mask_cast, 1)
            nc.vector.tensor_scalar(row_scale[:, :], mask_f[:, :], 0.0, SCALE, ALU.not_equal, ALU.mult)\
                .then_inc(mask_set, 1)
            dve.wait_ge(v_ones, 2)
            walk_tiles(dve, step, 4, 2)

            hid_bank = score_bank + pt_bank
            y_bank = [ot_bank, tail_bank]

            def hidden(j):
                for c in range(1, FCH, 2):
                    dve.wait_ge(hid_done[c], j.value(1))
                    if due(j.value(-1)):
                        dve.wait_ge(f_y_done, j.value(-1))
                    nc.vector.tensor_scalar(hidT[:, j.par, c, :], hid_bank[c][:, :], b_1[:, c:c + 1], 0.0,
                                            ALU.add, ALU.max).then_inc(hid_ready[c], 1)

            def group_norm(j):
                dve.wait_ge(f_y_done, j.value(1))
                dve.wait_ge(f_loaded[j.par], j.rounds(-2))
                nc.vector.tensor_tensor(f_y[:, :, :],
                                        y_bank[j.par][:, :].rearrange("p (t d) -> p t d", t=GROUP),
                                        f_in[:, j.par, :, :], ALU.add).then_inc(f_y_read, 1)
                dve.wait_ge(f_y_read, j.value(1))
                nc.vector.tensor_tensor(f_z[:, j.par, :, :], f_y[:, :, :],
                                        b_2[:, :].unsqueeze(1).to_broadcast([P, GROUP, D]), ALU.add)\
                    .then_inc(f_z_ready, 1)
                dve.wait_ge(f_z_ready, j.value(1))
                for t in range(GROUP):
                    last = nc.vector.bn_stats(f_stats[:, t, :], f_z[:, j.par, t, :])
                last.then_inc(f_stats_ready, 1)
                dve.wait_ge(v_ones, 2)
                dve.wait_ge(f_stats_ready, j.value(1))
                for t in range(GROUP):
                    last = nc.vector.bn_aggr(f_mv[:, j.par, t, :], f_stats[:, t, :])
                last.then_inc(f_mean_ready, 1)
                dve.wait_ge(f_mean_ready, j.value(1))
                nc.vector.tensor_scalar(f_ve[:, j.par, :], f_mv[:, j.par, :, 1], EPS, None, ALU.add)\
                    .then_inc(f_var_ready, 1)

            def group_finish(j):
                dve.wait_ge(f_rstd_ready, j.value(1))
                if due(j.value(-1)):
                    dve.wait_ge(f_gamma_done, j.value(-1))
                for t in range(GROUP):
                    last = nc.vector.tensor_scalar(f_norm[:, j.par, t, :], f_z[:, j.par, t, :],
                                                   f_mv[:, j.par, t, 0:1], f_rstd[:, j.par, t:t + 1],
                                                   ALU.subtract, ALU.mult)
                last.then_inc(f_norm_ready, 1)

            def group_step(j):
                if group_exists(j):
                    hidden(j)
                if group_exists(j - 1):
                    group_finish(j - 1)
                if group_exists(j):
                    group_norm(j)

            walk_groups(dve, group_step, 0, 1)

        @block.gpsimd
        def _(pool):
            def spread_keys(g):
                pool.wait_ge(k_ready, g.value(1))
                if due(g.value(-1)):
                    pool.wait_ge(scored[1], g.value(-1))
                for b in range(2):
                    keys = KT[:, g.slot, b * S:(b + 1) * S].unsqueeze(1).to_broadcast([P, HALF, S])
                    own = own_head[:, :].unsqueeze(2).to_broadcast([P, HALF, S])
                    last = nc.gpsimd.tensor_tensor(Kx[:, g.par, b, :, :], keys, own, ALU.mult)
                last.then_inc(k_spread, 1)

            def root(g):
                pool.wait_ge(var_ready, g.value(1))
                if due(g.value(1 - SLOTS)):
                    pool.wait_ge(norm_ready, g.value(1 - SLOTS))
                nc.gpsimd.tensor_tensor(rstd[:, g.slot:g.slot + 1], var_eps[:, g.slot:g.slot + 1],
                                        neg_half[:, 0:1], ALU.pow).then_inc(rstd_ready, 1)

            def bias_residual(g):
                pool.wait_ge(res_loaded[g.slot], g.rounds(-SLOTS))
                pool.wait_ge(z_ready, g.value(1 - SLOTS))
                nc.gpsimd.tensor_tensor(x_bias[:, g.slot, :], x_res[:, g.slot, :], b_o[:, g.layer, :], ALU.add)\
                    .then_inc(res_biased, 1)

            def scale(g):
                pool.wait_ge(norm_ready, g.value(1))
                if due(g.value()):
                    pool.wait_ge(out_ready, g.value())
                nc.gpsimd.tensor_tensor(scaled[:, :], normed[:, g.slot, :], ln_g[:, g.layer, :], ALU.mult)\
                    .then_inc(gamma_done, 1)
                if due(g.rounds()):
                    pool.wait_ge(stored[g.slot], g.rounds())
                pool.wait_ge(gamma_done, g.value(1))
                nc.gpsimd.tensor_tensor(x_out[:, g.slot, :], scaled[:, :], ln_b[:, g.layer, :], ALU.add)\
                    .then_inc(out_ready, 1)

            def step(i):
                if exists(i - 2):
                    root(i - 2)
                if exists(i + 2):
                    spread_keys(i + 2)
                if exists(i) and (i).layer:
                    bias_residual(i)
                if exists(i - 3):
                    scale(i - 3)

            nc.gpsimd.memset(ident[:, :], 0.0).then_inc(consts_zero, 1)
            nc.gpsimd.memset(head_mask[:, :, :], 1.0).then_inc(consts_zero, 1)
            nc.gpsimd.memset(neg_half[:, :], -0.5).then_inc(consts_zero, 1)
            nc.gpsimd.memset(ones_row[:, :], 1.0).then_inc(consts_zero, 1)
            pool.wait_ge(consts_zero, 4)
            nc.gpsimd.affine_select(out=ident[:, :], in_=ident[:, :], compare_op=ALU.not_equal, fill=1.0,
                                    base=0, pattern=[[-1, P]], channel_multiplier=1).then_inc(consts_set, 1)
            nc.gpsimd.affine_select(out=head_mask[:, :, :], in_=head_mask[:, :, :], compare_op=ALU.is_ge,
                                    fill=0.0, base=0, pattern=[[-DH * HALF, 2], [-DH, HALF]],
                                    channel_multiplier=1).then_inc(consts_band, 1)
            pool.wait_ge(consts_band, 1)
            nc.gpsimd.affine_select(out=head_mask[:, :, :], in_=head_mask[:, :, :], compare_op=ALU.is_ge,
                                    fill=0.0, base=DH - 1, pattern=[[DH * HALF, 2], [DH, HALF]],
                                    channel_multiplier=-1).then_inc(consts_band, 1)
            pool.wait_ge(consts_band, 2)
            nc.gpsimd.tensor_tensor(own_head[:, :], head_mask[:, 0, :], head_mask[:, 1, :], ALU.add)\
                .then_inc(consts_set, 1)
            pool.wait_ge(consts_set, 2)
            pool.wait_ge(loaded, LOADED)
            pool.wait_ge(loaded_late, LOADED_LATE)
            walk_tiles(pool, step, 3, 3)

            def group_root(j):
                pool.wait_ge(f_var_ready, j.value(1))
                if due(j.value(-1)):
                    pool.wait_ge(f_norm_ready, j.value(-1))
                nc.gpsimd.tensor_tensor(f_rstd[:, j.par, :], f_ve[:, j.par, :], neg_half[:, :], ALU.pow)\
                    .then_inc(f_rstd_ready, 1)

            def group_scale(j):
                pool.wait_ge(f_norm_ready, j.value(1))
                if due(j.value()):
                    pool.wait_ge(f_out_ready, j.value())
                gamma = ln_g[:, LAYERS, :].unsqueeze(1).to_broadcast([P, GROUP, D])
                beta = ln_b[:, LAYERS, :].unsqueeze(1).to_broadcast([P, GROUP, D])
                nc.gpsimd.tensor_tensor(f_scaled[:, :, :], f_norm[:, j.par, :, :], gamma, ALU.mult)\
                    .then_inc(f_gamma_done, 1)
                pool.wait_ge(f_gamma_done, j.value(1))
                if due(j.rounds()):
                    pool.wait_ge(f_stored[j.par], j.rounds())
                nc.gpsimd.tensor_tensor(f_out[:, j.par, :, :], f_scaled[:, :, :], beta, ALU.add)\
                    .then_inc(f_out_ready, 1)

            def group_step(j):
                if group_exists(j):
                    group_root(j)
                if group_exists(j - 1):
                    group_scale(j - 1)

            walk_groups(pool, group_step, 0, 1)


def kernel(**inputs):
    import concourse.bacc as bacc
    from concourse.bass_utils import run_bass_kernel_spmd

    nc = bacc.Bacc("TRN2", target_bir_lowering=False, num_devices=1)
    arrays, args = {}, {}
    for name, value in inputs.items():
        v = np.ascontiguousarray(value)
        if v.ndim == 3:
            v = v.reshape(B * S, D)
        arrays[name] = v
        args[name] = nc.dram_tensor(name, v.shape, mybir.dt.from_np(v.dtype), kind="ExternalInput").ap()
    out = nc.dram_tensor("out", (B * S, D), F32, kind="ExternalOutput").ap()
    mid = [nc.dram_tensor(f"layer{n}_out", (B * S, D), F32, kind="Internal").ap() for n in range(LAYERS)]
    build(nc, args, out, mid)
    got = run_bass_kernel_spmd(nc, [arrays], core_ids=[0])
    return got.results[0]["out"].reshape(B, S, D)
```

```python
from contextlib import ExitStack

import numpy as np

import concourse.bass as bass
from concourse import mybir

F32 = mybir.dt.float32
ALU = mybir.AluOpType
ACT = mybir.ActivationFunctionType
AX = mybir.AxisListType

B, S, D, H, FF = 128, 64, 128, 16, 512
DH = D // H
P = 128
TILES = B * S // P
LAYERS = 3
G = LAYERS * TILES
HALF = H // 2
PAIRS = HALF // 2
VC = DH + 1
EPS = 1e-5
SCALE = float(1.0 / np.sqrt(np.float32(DH)))
SLOTS = 4
UNROLL, EDGE = 8, 8
FCH = FF // P
PAIR_SLOTS = SLOTS // 2
GROUP = 4
GROUPS = TILES // GROUP
SELF, CROSS = 1, 2
FIRST_ROWS = TILES + 2
LATER_ROWS = 3 * (LAYERS - 1) + FCH


class At:

    def __init__(self, n, slots, r=None, step=0):
        self.n, self.slots, self.r, self.step = n, slots, r, step

    def __add__(self, k):
        return At(self.n + k, self.slots, self.r, self.step)

    def __sub__(self, k):
        return self + -k

    def value(self, k=0):
        return self.n + k if self.r is None else self.r * self.step + (self.n + k)

    def rounds(self, k=0):
        n = 16 * ((self.n - k) // self.slots)
        return n if self.r is None else self.r * (16 * self.step // self.slots) + n

    @property
    def pair(self):
        return self.n // 2 % PAIR_SLOTS

    def scaled(self, factor, k=0):
        n = self.n * factor + k
        return n if self.r is None else self.r * (self.step * factor) + n

    @property
    def layer(self):
        return self.n // TILES

    @property
    def slot(self):
        return self.n % SLOTS

    @property
    def par(self):
        return self.n % 2


def due(count):
    return not isinstance(count, int) or count >= 1


def walk_tiles(eng, step, start, stop):
    for n in range(start, EDGE):
        step(At(n, SLOTS))
    for layer in range(LAYERS):
        first, last = layer * TILES + EDGE, (layer + 1) * TILES - EDGE
        with eng.Fori(0, (last - first) // UNROLL) as r:
            for k in range(UNROLL):
                step(At(first + k, SLOTS, r, UNROLL))
        end = stop if layer == LAYERS - 1 else (layer + 1) * TILES + EDGE
        for n in range(last, end):
            step(At(n, SLOTS))


def walk_groups(eng, step, start, stop):
    for n in range(start, 4):
        step(At(n, 2))
    with eng.Fori(0, (GROUPS - 8) // 4) as r:
        for k in range(4):
            step(At(4 + k, 2, r, 4))
    for n in range(GROUPS - 4, stop):
        step(At(n, 2))


def exists(g):
    return 0 <= g.n < G


def group_exists(j):
    return 0 <= j.n < GROUPS


def build(nc, a, out):
    ctx = ExitStack()
    with ctx:
        def sb(name, shape, dt=F32):
            return ctx.enter_context(nc.sbuf_tensor(name, shape, dt))

        def bank(name):
            return ctx.enter_context(nc.psum_tensor(name, [P, 512], F32))

        def sem(name):
            return ctx.enter_context(nc.semaphore(name))

        ident = sb("ident", [P, P])
        head_mask = sb("head_mask", [P, 2, HALF])
        own_head = sb("own_head", [P, HALF])
        neg_half = sb("neg_half", [P, GROUP])
        w_q = sb("w_q", [P, LAYERS, D])
        w_k = sb("w_k", [P, LAYERS, D])
        w_v = sb("w_v", [P, LAYERS, D])
        w_o = sb("w_o", [P, LAYERS, D])
        first_rows = sb("first_rows", [FIRST_ROWS, P])
        later_rows = sb("later_rows", [LATER_ROWS, P])
        first_cols = sb("first_cols", [P, 2])
        later_cols = sb("later_cols", [P, LATER_ROWS])
        b_v_wide = sb("b_v_wide", [P, LAYERS - 1, P])
        neg_b_v = sb("neg_b_v", [P, H // 2, DH])
        b_o = sb("b_o", [P, LAYERS, D])
        ln_g = sb("ln_g", [P, LAYERS + 1, D])
        ln_b = sb("ln_b", [P, LAYERS + 1, D])
        w_1 = sb("w_1", [P, FF])
        w_2 = sb("w_2", [P, FCH, D])
        b_2 = sb("b_2", [P, D])
        mask_i = sb("mask_i", [TILES, P], mybir.dt.int32)
        row_scale = sb("row_scale", [P, TILES])

        state = sb("state", [P, TILES, D])
        cT = sb("cT", [P, TILES, P])

        x_in = sb("x_in", [P, SLOTS, D])
        c_in = sb("c_in", [P, SLOTS, D])
        xcT = sb("xcT", [P, SLOTS, 2, P])
        QT = sb("QT", [P, SLOTS, 2, P])
        KT = sb("KT", [P, SLOTS, P])
        Kx = sb("Kx", [P, 2, 2, HALF, S])
        Vx = sb("Vx", [P, SLOTS, 2, H // 2, 2, VC])
        row_max = sb("row_max", [P, 2, H])
        shifted = sb("shifted", [P, 2, 2, HALF, S])
        probs = sb("probs", [P, 2, 2, HALF * S])
        PT = sb("PT", [P, 2, 2, PAIRS, P])
        OT = sb("OT", [P, 2, 2, P])
        inv_sum = sb("inv_sum", [P, 2, H // 2, 2])
        attn = sb("attn", [P, 2, H, DH])
        attnT = sb("attnT", [P, 2, P])
        x_bias = sb("x_bias", [P, SLOTS, D])
        z = sb("z", [P, SLOTS, D])
        stats = sb("stats", [P, 6])
        mean_var = sb("mean_var", [P, SLOTS, 2])
        var_eps = sb("var_eps", [P, SLOTS])
        rstd = sb("rstd", [P, SLOTS])
        normed = sb("normed", [P, SLOTS, D])
        scaled = sb("scaled", [P, D])

        f_in = sb("f_in", [P, 2, GROUP, D])
        f_inT = sb("f_inT", [P, 2, GROUP * P])
        hidT = sb("hidT", [P, 2, FCH, GROUP * P])
        f_bias = sb("f_bias", [P, 2, GROUP, D])
        f_z = sb("f_z", [P, 2, GROUP, D])
        f_stats = sb("f_stats", [P, GROUP, 6])
        f_mv = sb("f_mv", [P, 2, GROUP, 2])
        f_ve = sb("f_ve", [P, 2, GROUP])
        f_rstd = sb("f_rstd", [P, 2, GROUP])
        f_norm = sb("f_norm", [P, 2, GROUP, D])
        f_scaled = sb("f_scaled", [P, GROUP, D])

        in_bank = bank("in_bank")
        proj_bank = bank("proj_bank")
        score_bank = [bank("score_bank0"), bank("score_bank1")]
        pt_bank = [bank("pt_bank0"), bank("pt_bank1")]
        ot_bank = bank("ot_bank")
        tail_bank = bank("tail_bank")

        loaded = sem("loaded")
        w_o_loaded = sem("w_o_loaded")
        first_norm_loaded = sem("first_norm_loaded")
        loaded_late = sem("loaded_late")
        consts_zero = sem("consts_zero")
        consts_band = sem("consts_band")
        consts_set = sem("consts_set")
        rows_loaded = sem("rows_loaded")
        mask_cast = sem("mask_cast")
        rows_turned = sem("rows_turned")
        later_rows_loaded = sem("later_rows_loaded")
        later_turned = sem("later_turned")
        later_cols_ready = sem("later_cols_ready")
        cols_ready = sem("cols_ready")
        b_v_spread = sem("b_v_spread")
        b_v_projected = sem("b_v_projected")
        b_o_ready = sem("b_o_ready")
        neg_b_v_set = sem("neg_b_v_set")
        q_zeroed = sem("q_zeroed")
        v_zeroed = sem("v_zeroed")
        ot_zeroed = sem("ot_zeroed")
        v_ones = sem("v_ones")
        x_loaded = [sem(f"x_loaded{s}") for s in range(PAIR_SLOTS)]
        c_loaded = [sem(f"c_loaded{s}") for s in range(PAIR_SLOTS)]
        state_loaded = [sem(f"state_loaded{s}") for s in range(PAIR_SLOTS)]
        cT_saved = [sem(f"cT_saved{s}") for s in range(PAIR_SLOTS)]
        cT_loaded = [sem(f"cT_loaded{s}") for s in range(PAIR_SLOTS)]
        in_transposed = sem("in_transposed")
        in_copied = sem("in_copied")
        projected = sem("projected")
        k_ready = sem("k_ready")
        q_ready = sem("q_ready")
        v_ready = sem("v_ready")
        k_spread = sem("k_spread")
        scored = [sem("scored0"), sem("scored1")]
        max_ready = [sem("max_ready0"), sem("max_ready1")]
        shift_ready = [sem("shift_ready0"), sem("shift_ready1")]
        exp_ready = [sem("exp_ready0"), sem("exp_ready1")]
        probs_transposed = [sem("probs_transposed0"), sem("probs_transposed1")]
        pt_copied = [sem("pt_copied0"), sem("pt_copied1")]
        pv_done = sem("pv_done")
        ot_copied = sem("ot_copied")
        o_back = sem("o_back")
        inv_ready = sem("inv_ready")
        attn_ready = sem("attn_ready")
        attn_transposed = sem("attn_transposed")
        attn_copied = sem("attn_copied")
        y_done = sem("y_done")
        tail_free = sem("tail_free")
        res_biased = sem("res_biased")
        z_ready = sem("z_ready")
        stats_ready = sem("stats_ready")
        mean_ready = sem("mean_ready")
        var_ready = sem("var_ready")
        rstd_ready = sem("rstd_ready")
        norm_ready = sem("norm_ready")
        gamma_done = sem("gamma_done")
        out_ready = sem("out_ready")
        f_loaded = [sem("f_loaded0"), sem("f_loaded1")]
        f_stored = sem("f_stored")
        f_transposed = sem("f_transposed")
        f_copied = sem("f_copied")
        hid_done = [sem(f"hid_done{c}") for c in range(FCH)]
        hid_ready = [sem(f"hid_ready{c}") for c in range(FCH)]
        f_y_done = sem("f_y_done")
        f_biased = sem("f_biased")
        f_z_ready = sem("f_z_ready")
        f_stats_ready = sem("f_stats_ready")
        f_mean_ready = sem("f_mean_ready")
        f_var_ready = sem("f_var_ready")
        f_rstd_ready = sem("f_rstd_ready")
        f_norm_ready = sem("f_norm_ready")
        f_gamma_done = sem("f_gamma_done")
        f_out_ready = sem("f_out_ready")
        last_gamma_done = sem("last_gamma_done")
        last_out_ready = sem("last_out_ready")

        block = ctx.enter_context(nc.Block())

        def tiles_of(t):
            return t.rearrange("(t p) d -> t p d", p=P)

        x_t, c_t, out_t = tiles_of(a["x"]), tiles_of(a["ctx_1024"]), tiles_of(out)

        def tiles_at(t, i, count):
            return t[i:i + count].rearrange("t p d -> p t d") if isinstance(i, int) else \
                t[bass.ds(i, count)].rearrange("t p d -> p t d")

        def state_at(i, count):
            return state[:, i:i + count, :] if isinstance(i, int) else state[:, bass.ds(i, count), :]

        def state_tile(g):
            return state_at(g.value(-g.layer * TILES), 1).rearrange("p t d -> p (t d)")

        def cT_at(i, count):
            return cT[:, i:i + count, :] if isinstance(i, int) else cT[:, bass.ds(i, count), :]

        def row(v):
            return v.rearrange("(a n) -> a n", a=1).to_broadcast([P, v.shape[0]])

        L1 = "L1_xattn_"
        kinds = ["L0_xattn_W", L1 + "sa_w", L1 + "ca_w"]
        biases = ["L0_xattn_b", L1 + "sa_b", L1 + "ca_b"]
        first_rows_loads = [(first_rows[TILES:TILES + 1, :], a[biases[0] + "k"].rearrange("(a n) -> a n", a=1)),
                            (first_rows[TILES + 1:TILES + 2, :],
                             a[biases[0] + "q"].rearrange("(a n) -> a n", a=1)),
                            (mask_i[:, :], a["mask_BxS2_ik0"].rearrange("(t b) s -> t (b s)", b=P // S))]
        later_rows_loads = [(later_rows[m * (LAYERS - 1) + n - 1:m * (LAYERS - 1) + n, :],
                             a[biases[n] + kind].rearrange("(a n) -> a n", a=1))
                            for m, kind in enumerate("kqv") for n in range(1, LAYERS)]
        later_rows_loads += [(later_rows[LATER_ROWS - FCH:LATER_ROWS, :],
                              a[L1 + "ff_b1"].rearrange("(c p) -> c p", p=P))]

        def b_k(layer):
            return later_cols[:, layer - 1:layer] if layer else first_cols[:, 0:1]

        def b_q(layer):
            return later_cols[:, LAYERS - 2 + layer:LAYERS - 1 + layer] if layer else first_cols[:, 1:2]

        b_v, b_1 = later_cols[:, 2 * (LAYERS - 1):], later_cols[:, 3 * (LAYERS - 1):]
        sp_first = [(w_k[:, 0, :], a[kinds[0] + "k"]), (w_q[:, 0, :], a[kinds[0] + "q"]),
                    (b_o[:, 0, :], row(a[biases[0] + "v"]))]
        act_first = [(w_v[:, 0, :], a[kinds[0] + "v"])]
        out_projections, late = [], []
        for n in range(1, LAYERS):
            out_projections += [(w_o[:, n, :], a[kinds[n] + "o"]), (b_o[:, n, :], row(a[biases[n] + "o"]))]
        for n, (g, b) in enumerate([("L0_xattn_gamma", "L0_xattn_beta")] +
                                   [(L1 + f"ln{i}_g", L1 + f"ln{i}_b") for i in (1, 2, 3)]):
            late += [(ln_g[:, n, :], row(a[g])), (ln_b[:, n, :], row(a[b]))]
        for n in range(1, LAYERS):
            late += [(w_k[:, n, :], a[kinds[n] + "k"]), (w_q[:, n, :], a[kinds[n] + "q"]),
                     (w_v[:, n, :], a[kinds[n] + "v"])]
        first_norm, late = late[:2], late[2:]
        late += [(w_1[:, :], a[L1 + "ff_w1"]),
                 (w_2[:, :, :], a[L1 + "ff_w2"].rearrange("(c p) n -> p c n", p=P)),
                 (b_2[:, :], row(a[L1 + "ff_b2"]))]
        LOADED, LOADED_LATE, ROWS_LOADED = 16 * len(sp_first + act_first), 16 * len(late), \
            16 * len(first_rows_loads)
        LATER_ROWS_LOADED = 16 * len(later_rows_loads)
        W_O_LOADED = 16 * len(out_projections)

        @block.sync
        def _(sp):
            def long_met(g):
                if g.r is not None:
                    sp.wait_ge(in_copied, 1)

            def load_pair(g):
                tile = g.value(-g.layer * TILES)
                slots = slice(2 * g.pair, 2 * g.pair + 2)
                long_met(g)
                if due(g.value(2 - SLOTS)):
                    sp.wait_ge(in_transposed, g.value(2 - SLOTS))
                if g.layer:
                    sp.dma_start(x_in[:, slots, :], state_at(tile, 2)).then_inc(x_loaded[g.pair], 16)
                else:
                    sp.dma_start(x_in[:, slots, :], tiles_at(x_t, tile, 2)).then_inc(x_loaded[g.pair], 16)
                    sp.dma_start(c_in[:, slots, :], tiles_at(c_t, tile, 2)).then_inc(c_loaded[g.pair], 16)

            def load_state(g):
                long_met(g)
                if due(g.value(2 - SLOTS)):
                    sp.wait_ge(res_biased, g.value(2 - SLOTS))
                sp.dma_start(state_at(g.value(), 2), tiles_at(x_t, g.value(), 2))\
                    .then_inc(state_loaded[g.pair], 16)

            def save_cT(g):
                long_met(g)
                sp.wait_ge(in_copied, g.value(2))
                sp.dma_start(cT_at(g.value(), 2), xcT[:, 2 * g.pair:2 * g.pair + 2, 1, :])\
                    .then_inc(cT_saved[g.pair], 16)

            def load_cT(g):
                long_met(g)
                for s in range(PAIR_SLOTS):
                    sp.wait_ge(cT_saved[s], 16 * TILES // SLOTS)
                sp.wait_ge(projected, g.value(2 - SLOTS))
                sp.dma_start(xcT[:, 2 * g.pair:2 * g.pair + 2, 1, :], cT_at(g.value(-CROSS * TILES), 2))\
                    .then_inc(cT_loaded[g.pair], 16)

            def step(i):
                if i.n % 2:
                    return
                if exists(i + 6):
                    load_pair(i + 6)
                if exists(i + 2) and (i + 2).layer == 0:
                    save_cT(i + 2)
                if exists(i + 4) and (i + 4).layer == CROSS:
                    load_cT(i + 4)
                if exists(i + 4) and (i + 4).layer == 0:
                    load_state(i + 4)

            def load_group(j):
                sp.wait_ge(out_ready, G if j.n >= 4 else j.scaled(GROUP, (LAYERS - 1) * TILES + GROUP))
                if due(j.value(-1)):
                    sp.wait_ge(f_biased, j.value(-1))
                sp.dma_start(f_in[:, j.par, :, :], state_at(j.scaled(GROUP), GROUP))\
                    .then_inc(f_loaded[j.par], 16)

            def store_group(j):
                long_met(j)
                if j.n == GROUPS - 1:
                    sp.wait_ge(last_out_ready, 1)
                else:
                    sp.wait_ge(f_out_ready, j.value(1))
                sp.dma_start(tiles_at(out_t, j.scaled(GROUP), GROUP), state_at(j.scaled(GROUP), GROUP))\
                    .then_inc(f_stored, 16)

            def group_step(j):
                if group_exists(j + 2):
                    load_group(j + 2)
                if group_exists(j - 2):
                    store_group(j - 2)

            load_pair(At(0, SLOTS))
            for dst, src in sp_first:
                sp.dma_start(dst, src).then_inc(loaded, 16)
            load_pair(At(2, SLOTS))
            load_state(At(0, SLOTS))
            for dst, src in later_rows_loads:
                sp.dma_start(dst, src).then_inc(later_rows_loaded, 16)
            for dst, src in out_projections:
                sp.dma_start(dst, src).then_inc(w_o_loaded, 16)
            for dst, src in first_norm:
                sp.dma_start(dst, src).then_inc(first_norm_loaded, 16)
            for n in range(-2, 3):
                step(At(n, SLOTS))
            for dst, src in late:
                sp.dma_start(dst, src).then_inc(loaded_late, 16)
            walk_tiles(sp, step, 3, G)
            walk_groups(sp, group_step, -2, GROUPS + 2)
            sp.wait_ge(f_stored, 16 * GROUPS)

        @block.tensor
        def _(pe):
            def transpose_inputs(g):
                if g.n % 2 == 0:
                    pe.wait_ge(x_loaded[g.pair], g.rounds(-SLOTS))
                    if g.layer == 0:
                        pe.wait_ge(c_loaded[g.pair], g.rounds(-SLOTS))
                if due(g.value()):
                    pe.wait_ge(in_copied, g.value())
                last = nc.tensor.transpose(in_bank[:, 0:P], x_in[:, g.slot, :], ident[:, :])
                if g.layer == 0:
                    last = nc.tensor.transpose(in_bank[:, P:2 * P], c_in[:, g.slot, :], ident[:, :])
                last.then_inc(in_transposed, 1)

            def project(g):
                kv = 0 if g.layer == SELF else 1
                if g.n == TILES:
                    pe.wait_ge(loaded_late, LOADED_LATE)
                if g.layer == CROSS and g.n % 2 == 0:
                    pe.wait_ge(cT_loaded[g.pair], g.rounds(-SLOTS + CROSS * TILES))
                pe.wait_ge(in_copied, g.value(1))
                if due(g.value()):
                    pe.wait_ge(v_ready, g.value())
                q_src, kv_src = xcT[:, g.slot, 0, :], xcT[:, g.slot, kv, :]
                nc.tensor.matmul(proj_bank[:, P:2 * P], w_k[:, g.layer, :], kv_src, start=True, stop=True)
                nc.tensor.matmul(proj_bank[:, 0:P], w_q[:, g.layer, :], q_src, start=True, stop=True)
                for b in range(2):
                    for e in range(2):
                        heads = w_v[:, g.layer, :].rearrange("p (c e d) -> p e c d", e=2, d=DH)[:, e, :, :]
                        last = nc.tensor.matmul(proj_bank[e * S:(e + 1) * S, 2 * P + b * S:2 * P + (b + 1) * S],
                                                kv_src[:, b * S:(b + 1) * S], heads, start=True, stop=True)
                last.then_inc(projected, 1)

            def score(g, h):
                pe.wait_ge(q_ready, g.value(1))
                pe.wait_ge(k_spread, g.value(1))
                if due(g.value()):
                    pe.wait_ge(shift_ready[h], g.value())
                for b in range(2):
                    last = nc.tensor.matmul(score_bank[h][b * S:(b + 1) * S, :],
                                            QT[:, g.slot, h, b * S:(b + 1) * S],
                                            Kx[:, g.par, b, :, :],
                                            start=True, stop=True)
                last.then_inc(scored[h], 1)

            def transpose_probs(g, h):
                pe.wait_ge(exp_ready[h], g.value(1))
                if due(g.value()):
                    pe.wait_ge(pt_copied[h], g.value())
                for c in range(PAIRS):
                    last = nc.tensor.transpose(pt_bank[h][:, c * P:(c + 1) * P],
                                               probs[:, g.par, h, c * P:(c + 1) * P], ident[:, :])
                last.then_inc(probs_transposed[h], 1)

            def weigh_values(g, h):
                pe.wait_ge(pt_copied[h], g.value(1))
                if h == 0:
                    pe.wait_ge(v_ready, g.value(1))
                    if due(g.value()):
                        pe.wait_ge(ot_copied, g.value())
                    else:
                        pe.wait_ge(ot_zeroed, 1)
                for b in range(2):
                    for c in range(PAIRS):
                        last = nc.tensor.matmul(
                            ot_bank[32 * c:32 * c + 2 * VC, h * P + b * S:h * P + (b + 1) * S],
                            Vx[:, g.slot, b, h * PAIRS + c, :, :],
                            PT[:, g.par, h, c, b * S:(b + 1) * S], start=True, stop=True)
                if h == 1:
                    last.then_inc(pv_done, 1)

            def transpose_back(g):
                pe.wait_ge(ot_copied, g.value(1))
                if g.n == 0:
                    pe.wait_ge(b_o_ready, LAYERS - 1)
                if g.n and (g - 1).layer == 0 and due(g.value()):
                    pe.wait_ge(tail_free, g.value())
                elif g.n:
                    pe.wait_ge(z_ready, g.value())
                for h in range(2):
                    last = nc.tensor.transpose(tail_bank[:, h * P:(h + 1) * P], OT[:, g.par, h, :],
                                               ident[:, :])
                last.then_inc(o_back, 1)

            def transpose_attn(g):
                pe.wait_ge(attn_ready, g.value(1 - TILES))
                nc.tensor.transpose(tail_bank[:, 2 * P:3 * P], attn[:, g.par, :, :], ident[:, :])\
                    .then_inc(attn_transposed, 1)

            def project_out(g):
                pe.wait_ge(attn_copied, g.value(1 - TILES))
                nc.tensor.matmul(tail_bank[:, 3 * P:4 * P], attnT[:, g.par, :], w_o[:, g.layer, :],
                                 start=True, stop=True).then_inc(y_done, 1)

            def step(i):
                if exists(i + 1):
                    score(i + 1, 0)
                if exists(i):
                    transpose_probs(i, 0)
                if exists(i - 1):
                    transpose_back(i - 1)
                if exists(i + 1):
                    score(i + 1, 1)
                if exists(i):
                    transpose_probs(i, 1)
                if exists(i - 1) and (i - 1).layer:
                    transpose_attn(i - 1)
                if exists(i + 3):
                    project(i + 3)
                if exists(i):
                    weigh_values(i, 0)
                if exists(i):
                    weigh_values(i, 1)
                if exists(i + 4):
                    transpose_inputs(i + 4)
                if exists(i - 1) and (i - 1).layer:
                    project_out(i - 1)

            def turn_rows():
                pe.wait_ge(mask_cast, 1)
                pe.wait_ge(rows_loaded, ROWS_LOADED)
                nc.tensor.transpose(tail_bank[:, 0:FIRST_ROWS], first_rows[:, :],
                                    ident[0:FIRST_ROWS, 0:FIRST_ROWS])\
                    .then_inc(rows_turned, 1)

            def turn_later_rows():
                pe.wait_ge(later_rows_loaded, LATER_ROWS_LOADED)
                pe.wait_ge(cols_ready, 2)
                nc.tensor.transpose(tail_bank[:, 0:LATER_ROWS], later_rows[:, :],
                                    ident[0:LATER_ROWS, 0:LATER_ROWS]).then_inc(later_turned, 1)

            def project_b_v():
                pe.wait_ge(w_o_loaded, W_O_LOADED)
                pe.wait_ge(later_cols_ready, 1)
                pe.wait_ge(b_v_spread, LAYERS - 1)
                for n in range(1, LAYERS):
                    nc.tensor.matmul(tail_bank[:, n * P:(n + 1) * P], b_v_wide[:, n - 1, :], w_o[:, n, :],
                                     start=True, stop=True).then_inc(b_v_projected, 1)

            pe.wait_ge(consts_set, 1)
            transpose_inputs(At(0, SLOTS))
            turn_rows()
            pe.wait_ge(loaded, LOADED)
            for n in range(-3, 0):
                step(At(n, SLOTS))
            turn_later_rows()
            step(At(0, SLOTS))
            project_b_v()
            walk_tiles(pe, step, 1, G)

            hid_bank = score_bank + pt_bank
            y_bank = [ot_bank, tail_bank]

            def transpose_group(j):
                pe.wait_ge(f_loaded[j.par], j.rounds(-2))
                if j.n:
                    pe.wait_ge(f_copied, j.value())
                else:
                    pe.wait_ge(in_copied, G)
                for t in range(GROUP):
                    last = nc.tensor.transpose(in_bank[:, t * P:(t + 1) * P], f_in[:, j.par, t, :],
                                               ident[:, :])
                last.then_inc(f_transposed, 1)

            def hidden(j):
                pe.wait_ge(f_copied, j.value(1))
                for c in range(FCH):
                    if j.n:
                        pe.wait_ge(hid_ready[c], j.value())
                    elif c < 2:
                        pe.wait_ge(shift_ready[c], G)
                    else:
                        pe.wait_ge(pt_copied[c - 2], G)
                    nc.tensor.matmul(hid_bank[c][:, :], w_1[:, c * P:(c + 1) * P], f_inT[:, j.par, :],
                                     start=True, stop=True).then_inc(hid_done[c], 1)

            def down(j):
                if j.n >= 2:
                    pe.wait_ge(f_z_ready, j.value(-1))
                elif j.n:
                    pe.wait_ge(z_ready, G)
                for c in range(FCH):
                    pe.wait_ge(hid_ready[c], j.value(1))
                for t in range(GROUP):
                    for c in range(FCH):
                        last = nc.tensor.matmul(y_bank[j.par][:, t * P:(t + 1) * P],
                                                hidT[:, j.par, c, t * P:(t + 1) * P], w_2[:, c, :],
                                                start=(c == 0), stop=(c == FCH - 1))
                last.then_inc(f_y_done, 1)

            def group_step(j):
                if group_exists(j):
                    hidden(j)
                if group_exists(j + 1):
                    transpose_group(j + 1)
                if group_exists(j - 1):
                    down(j - 1)

            last_tile = At(G - 1, SLOTS)
            transpose_group(At(0, 2))
            transpose_back(last_tile)
            hidden(At(0, 2))
            transpose_attn(last_tile)
            transpose_group(At(1, 2))
            project_out(last_tile)
            walk_groups(pe, group_step, 1, GROUPS + 1)

        @block.scalar
        def _(act):
            def copy_inputs(g):
                n = 2 if g.layer == 0 else 1
                act.wait_ge(in_transposed, g.value(1))
                if due(g.value(1 - SLOTS)):
                    act.wait_ge(projected, g.value(1 - SLOTS))
                if g.layer == 0 and due(g.rounds()):
                    act.wait_ge(cT_saved[g.pair], g.rounds())
                nc.scalar.activation(xcT[:, g.slot, 0:n, :].rearrange("p n t -> p (n t)"),
                                     in_bank[:, 0:n * P], ACT.Copy).then_inc(in_copied, 1)

            def exponentials(g, h):
                if g.layer == 0:
                    act.wait_ge(cols_ready, 2)
                act.wait_ge(shift_ready[h], g.value(1))
                if due(g.value(-1)):
                    act.wait_ge(probs_transposed[h], g.value(-1))
                if g.layer:
                    scale = SCALE
                elif g.r is None:
                    scale = row_scale[:, g.n:g.n + 1]
                else:
                    scale = row_scale[:, bass.ds(g.value(), 1)]
                nc.scalar.activation(probs[:, g.par, h, :],
                                     shifted[:, g.par, h, :, :].rearrange("p h k -> p (h k)"),
                                     ACT.Exp, scale=scale).then_inc(exp_ready[h], 1)

            def take_keys(g):
                if g.n == TILES:
                    act.wait_ge(later_cols_ready, 1)
                act.wait_ge(projected, g.value(1))
                if due(g.value(1 - SLOTS)):
                    act.wait_ge(k_spread, g.value(1 - SLOTS))
                nc.scalar.activation(KT[:, g.slot, :], proj_bank[:, P:2 * P],
                                     ACT.Relu if g.layer == 0 else ACT.Identity,
                                     bias=b_k(g.layer)).then_inc(k_ready, 1)

            def take_queries(g):
                act.wait_ge(projected, g.value(1))
                if due(g.value(1 - SLOTS)):
                    act.wait_ge(scored[1], g.value(1 - SLOTS))
                for h in range(2):
                    rows = slice(h * HALF * DH, (h + 1) * HALF * DH)
                    last = nc.scalar.activation(QT[rows, g.slot, h, :], proj_bank[rows, 0:P],
                                                ACT.Relu if g.layer == 0 else ACT.Identity,
                                                bias=b_q(g.layer)[rows, :])
                last.then_inc(q_ready, 1)

            def take_values(g):
                act.wait_ge(projected, g.value(1))
                act.wait_ge(pv_done, g.value(1 - SLOTS))
                for e in range(2):
                    rows = slice(e * S, (e + 1) * S)
                    last = nc.scalar.activation(
                        Vx[rows, g.slot, :, :, e, 0:DH],
                        proj_bank[rows, 2 * P:3 * P].rearrange("p (b c d) -> p b c d", b=2, d=DH), ACT.Identity)
                last.then_inc(v_ready, 1)

            def copy_pt(g, h):
                act.wait_ge(probs_transposed[h], g.value(1))
                if due(g.value(-1)):
                    act.wait_ge(pv_done, g.value(-1))
                nc.scalar.activation(PT[:, g.par, h, :, :].rearrange("p c q -> p (c q)"),
                                     pt_bank[h][:, :], ACT.Copy).then_inc(pt_copied[h], 1)

            def copy_ot(g):
                act.wait_ge(pv_done, g.value(1))
                if due(g.value(-1)):
                    act.wait_ge(o_back, g.value(-1))
                nc.scalar.activation(OT[:, g.par, :, :].rearrange("p h q -> p (h q)"),
                                     ot_bank[:, 0:2 * P], ACT.Copy).then_inc(ot_copied, 1)

            def copy_attn(g):
                act.wait_ge(attn_transposed, g.value(1 - TILES))
                if due(g.value(-1 - TILES)):
                    act.wait_ge(y_done, g.value(-1 - TILES))
                nc.scalar.activation(attnT[:, g.par, :], tail_bank[:, 2 * P:3 * P], ACT.Copy)\
                    .then_inc(attn_copied, 1)

            def step(i):
                if exists(i):
                    copy_pt(i, 0)
                if exists(i):
                    copy_pt(i, 1)
                if exists(i - 1) and (i - 1).layer:
                    copy_attn(i - 1)
                if exists(i + 1):
                    exponentials(i + 1, 0)
                if exists(i + 3):
                    take_keys(i + 3)
                if exists(i + 3):
                    take_queries(i + 3)
                if exists(i):
                    copy_ot(i)
                if exists(i + 3) and (i + 3).layer:
                    take_values(i + 3)
                if exists(i + 4):
                    copy_inputs(i + 4)
                if exists(i + 1):
                    exponentials(i + 1, 1)

            for dst, src in first_rows_loads:
                act.dma_start(dst, src).then_inc(rows_loaded, 16)
            for dst, src in act_first:
                act.dma_start(dst, src).then_inc(loaded, 16)
            act.wait_ge(q_zeroed, 1)
            act.wait_ge(v_ones, 2)
            copy_inputs(At(0, SLOTS))
            act.wait_ge(cols_ready, 2)
            walk_tiles(act, step, -3, G)

            hid_bank = score_bank + pt_bank

            def copy_group(j):
                act.wait_ge(f_transposed, j.value(1))
                if due(j.value(-1)):
                    act.wait_ge(hid_done[FCH - 1], j.value(-1))
                nc.scalar.activation(f_inT[:, j.par, :], in_bank[:, :], ACT.Copy).then_inc(f_copied, 1)

            def hidden(j):
                for c in range(0, FCH, 2):
                    act.wait_ge(hid_done[c], j.value(1))
                    if due(j.value(-1)):
                        act.wait_ge(f_y_done, j.value(-1))
                    nc.scalar.activation(hidT[:, j.par, c, :], hid_bank[c][:, :], ACT.Relu,
                                         bias=b_1[:, c:c + 1]).then_inc(hid_ready[c], 1)

            def group_step(j):
                if group_exists(j):
                    hidden(j)
                if group_exists(j + 1):
                    copy_group(j + 1)

            copy_group(At(0, 2))
            hidden(At(0, 2))
            copy_attn(At(G - 1, SLOTS))
            copy_group(At(1, 2))
            walk_groups(act, group_step, 1, GROUPS)

        @block.vector
        def _(dve):
            def maxima(g, h):
                dve.wait_ge(scored[h], g.value(1))
                nc.vector.tensor_reduce(row_max[:, g.par, h * HALF:(h + 1) * HALF],
                                        score_bank[h][:, :].rearrange("p (h k) -> p h k", k=S),
                                        AX.X, ALU.max).then_inc(max_ready[h], 1)

            def shift(g, h):
                dve.wait_ge(max_ready[h], g.value(1))
                if due(g.value(-1)):
                    dve.wait_ge(exp_ready[h], g.value(-1))
                top = row_max[:, g.par, h * HALF:(h + 1) * HALF].unsqueeze(2).to_broadcast([P, HALF, S])
                nc.vector.tensor_tensor(shifted[:, g.par, h, :, :],
                                        score_bank[h][:, :].rearrange("p (h k) -> p h k", k=S),
                                        top, ALU.subtract).then_inc(shift_ready[h], 1)

            def tail_view():
                pairs = tail_bank[:, 0:2 * P].rearrange("p (c v) -> p c v", v=32)
                return pairs[:, :, 0:2 * VC].rearrange("p c (e v) -> p c e v", v=VC)

            def invert(g):
                dve.wait_ge(o_back, g.value(1))
                nc.vector.reciprocal(inv_sum[:, g.par, :, :], tail_view()[:, :, :, DH]).then_inc(inv_ready, 1)

            def normalise(g):
                dve.wait_ge(inv_ready, g.value(1))
                inv = inv_sum[:, g.par, :, :].unsqueeze(3).to_broadcast([P, H // 2, 2, DH])
                if g.layer:
                    if due(g.value(-1 - TILES)):
                        dve.wait_ge(attn_transposed, g.value(-1 - TILES))
                nc.vector.tensor_tensor(attn[:, g.par, :, :].rearrange("p (c e) d -> p c e d", e=2),
                                        tail_view()[:, :, :, 0:DH], inv, ALU.mult)\
                    .then_inc(attn_ready if g.layer else tail_free, 1)

            def residual(g):
                if due(g.value(1 - SLOTS)):
                    dve.wait_ge(norm_ready, g.value(1 - SLOTS))
                dve.wait_ge(res_biased, g.value(1))
                if g.layer == 0:
                    dve.wait_ge(tail_free, g.value(1))
                    nc.vector.tensor_tensor(z[:, g.slot, :], attn[:, g.par, :, :].rearrange("p h d -> p (h d)"),
                                            x_bias[:, g.slot, :], ALU.add).then_inc(z_ready, 1)
                else:
                    dve.wait_ge(y_done, g.value(1 - TILES))
                    nc.vector.tensor_tensor(z[:, g.slot, :], tail_bank[:, 3 * P:4 * P], x_bias[:, g.slot, :],
                                            ALU.add).then_inc(z_ready, 1)

            def take_values(g):
                dve.wait_ge(q_ready, g.value(1))
                if due(g.value(1 - SLOTS)):
                    dve.wait_ge(pv_done, g.value(1 - SLOTS))
                for e in range(2):
                    rows = slice(e * S, (e + 1) * S)
                    last = nc.vector.tensor_tensor(
                        Vx[rows, g.slot, :, :, e, 0:DH],
                        proj_bank[rows, 2 * P:3 * P].rearrange("p (b c d) -> p b c d", b=2, d=DH),
                        neg_b_v[rows, :, :].unsqueeze(1).to_broadcast([S, 2, H // 2, DH]), ALU.max)
                last.then_inc(v_ready, 1)

            def moments(g):
                dve.wait_ge(z_ready, g.value(1))
                nc.vector.bn_stats(stats[:, :], z[:, g.slot, :]).then_inc(stats_ready, 1)

            def mean(g):
                dve.wait_ge(v_ones, 2)
                dve.wait_ge(stats_ready, g.value(1))
                nc.vector.bn_aggr(mean_var[:, g.slot, :], stats[:, :]).then_inc(mean_ready, 1)

            def add_eps(g):
                dve.wait_ge(mean_ready, g.value(1))
                nc.vector.tensor_scalar(var_eps[:, g.slot:g.slot + 1], mean_var[:, g.slot, 1:2], EPS, None,
                                        ALU.add).then_inc(var_ready, 1)

            def layer_norm(g):
                dve.wait_ge(rstd_ready, g.value(1))
                if due(g.value(1 - SLOTS)):
                    dve.wait_ge(gamma_done, g.value(1 - SLOTS))
                nc.vector.tensor_scalar(normed[:, g.slot, :], z[:, g.slot, :], mean_var[:, g.slot, 0:1],
                                        rstd[:, g.slot:g.slot + 1], ALU.subtract, ALU.mult)\
                    .then_inc(norm_ready, 1)

            def step(i):
                if exists(i + 1):
                    maxima(i + 1, 0)
                if exists(i - 1):
                    invert(i - 1)
                if exists(i - 1):
                    normalise(i - 1)
                if exists(i + 1):
                    shift(i + 1, 0)
                if exists(i + 1):
                    maxima(i + 1, 1)
                if exists(i - 2):
                    layer_norm(i - 2)
                if exists(i + 1):
                    shift(i + 1, 1)
                if exists(i - 1):
                    residual(i - 1)
                if exists(i - 1):
                    moments(i - 1)
                if exists(i + 3) and (i + 3).layer == 0:
                    take_values(i + 3)
                if exists(i - 1):
                    mean(i - 1)
                if exists(i - 1):
                    add_eps(i - 1)

            nc.vector.memset(Vx[:, :, :, :, :, :].rearrange("p s b c e v -> p (s b c e v)"), 0.0)\
                .then_inc(v_zeroed, 1)
            nc.vector.memset(QT[:, :, :, :].rearrange("p s h t -> p (s h t)"), 0.0).then_inc(q_zeroed, 1)
            nc.vector.memset(ot_bank[:, 0:2 * P], 0.0).then_inc(ot_zeroed, 1)
            dve.wait_ge(v_zeroed, 1)
            for e in range(2):
                nc.vector.memset(Vx[e * S:(e + 1) * S, :, :, :, e, DH:DH + 1]
                                 .rearrange("p s b c v -> p (s b c v)"), 1.0).then_inc(v_ones, 1)
            dve.wait_ge(rows_loaded, ROWS_LOADED)
            nc.vector.tensor_copy(first_rows[0:TILES, :], mask_i[:, :]).then_inc(mask_cast, 1)
            dve.wait_ge(rows_turned, 1)
            nc.vector.tensor_scalar(row_scale[:, :], tail_bank[:, 0:TILES], 0.0, SCALE, ALU.not_equal,
                                    ALU.mult).then_inc(cols_ready, 1)
            nc.vector.tensor_copy(first_cols[:, :], tail_bank[:, TILES:FIRST_ROWS]).then_inc(cols_ready, 1)
            dve.wait_ge(loaded, LOADED)
            for e in range(2):
                rows = slice(e * S, (e + 1) * S)
                heads = b_o[:, 0, :].rearrange("p (c e d) -> p e c d", e=2, d=DH)[rows, e, :, :]
                nc.vector.tensor_scalar(neg_b_v[rows, :, :], heads, -1.0, None, ALU.mult)\
                    .then_inc(neg_b_v_set, 1)
            dve.wait_ge(v_ones, 2)
            dve.wait_ge(neg_b_v_set, 2)
            for n in range(-3, 0):
                step(At(n, SLOTS))
            dve.wait_ge(later_turned, 1)
            nc.vector.tensor_copy(later_cols[:, :], tail_bank[:, 0:LATER_ROWS]).then_inc(later_cols_ready, 1)
            dve.wait_ge(later_cols_ready, 1)
            for n in range(LAYERS - 1):
                nc.vector.tensor_copy(b_v_wide[:, n, :], b_v[:, n:n + 1].to_broadcast([P, P]))\
                    .then_inc(b_v_spread, 1)
            step(At(0, SLOTS))
            for n in range(1, LAYERS):
                dve.wait_ge(b_v_projected, LAYERS - 1)
                nc.vector.tensor_tensor(b_o[:, n, :], tail_bank[:, n * P:(n + 1) * P], b_o[:, n, :], ALU.add)\
                    .then_inc(b_o_ready, 1)
            walk_tiles(dve, step, 1, G)

            hid_bank = score_bank + pt_bank
            y_bank = [ot_bank, tail_bank]

            def hidden(j):
                for c in range(1, FCH, 2):
                    dve.wait_ge(hid_done[c], j.value(1))
                    if due(j.value(-1)):
                        dve.wait_ge(f_y_done, j.value(-1))
                    nc.vector.tensor_scalar(hidT[:, j.par, c, :], hid_bank[c][:, :], b_1[:, c:c + 1], 0.0,
                                            ALU.add, ALU.max).then_inc(hid_ready[c], 1)

            def group_norm(j):
                dve.wait_ge(f_y_done, j.value(1))
                dve.wait_ge(f_biased, j.value(1))
                if due(j.value(-1)):
                    dve.wait_ge(f_norm_ready, j.value(-1))
                nc.vector.tensor_tensor(f_z[:, j.par, :, :],
                                        y_bank[j.par][:, :].rearrange("p (t d) -> p t d", t=GROUP),
                                        f_bias[:, j.par, :, :], ALU.add).then_inc(f_z_ready, 1)
                dve.wait_ge(f_z_ready, j.value(1))
                for t in range(GROUP):
                    last = nc.vector.bn_stats(f_stats[:, t, :], f_z[:, j.par, t, :])
                last.then_inc(f_stats_ready, 1)
                dve.wait_ge(v_ones, 2)
                dve.wait_ge(f_stats_ready, j.value(1))
                for t in range(GROUP):
                    last = nc.vector.bn_aggr(f_mv[:, j.par, t, :], f_stats[:, t, :])
                last.then_inc(f_mean_ready, 1)
                dve.wait_ge(f_mean_ready, j.value(1))
                nc.vector.tensor_scalar(f_ve[:, j.par, :], f_mv[:, j.par, :, 1], EPS, None, ALU.add)\
                    .then_inc(f_var_ready, 1)

            def group_finish(j):
                dve.wait_ge(f_rstd_ready, j.value(1))
                if due(j.value(-1)):
                    dve.wait_ge(f_gamma_done, j.value(-1))
                for t in range(GROUP):
                    last = nc.vector.tensor_scalar(f_norm[:, j.par, t, :], f_z[:, j.par, t, :],
                                                   f_mv[:, j.par, t, 0:1], f_rstd[:, j.par, t:t + 1],
                                                   ALU.subtract, ALU.mult)
                last.then_inc(f_norm_ready, 1)

            def group_step(j):
                if group_exists(j):
                    hidden(j)
                if group_exists(j - 2):
                    group_finish(j - 2)
                if group_exists(j - 1):
                    group_norm(j - 1)

            invert(At(G - 1, SLOTS))
            normalise(At(G - 1, SLOTS))
            layer_norm(At(G - 2, SLOTS))
            hidden(At(0, 2))
            residual(At(G - 1, SLOTS))
            moments(At(G - 1, SLOTS))
            mean(At(G - 1, SLOTS))
            add_eps(At(G - 1, SLOTS))
            layer_norm(At(G - 1, SLOTS))
            walk_groups(dve, group_step, 1, GROUPS + 2)
            last_group = At(GROUPS - 1, 2)
            gamma = ln_g[:, LAYERS, :].unsqueeze(1).to_broadcast([P, GROUP, D])
            beta = ln_b[:, LAYERS, :].unsqueeze(1).to_broadcast([P, GROUP, D])
            dve.wait_ge(f_norm_ready, GROUPS)
            dve.wait_ge(loaded_late, LOADED_LATE)
            nc.vector.tensor_tensor(f_bias[:, last_group.par, :, :], f_norm[:, last_group.par, :, :], gamma,
                                    ALU.mult).then_inc(last_gamma_done, 1)
            dve.wait_ge(last_gamma_done, 1)
            nc.vector.tensor_tensor(state_at(TILES - GROUP, GROUP), f_bias[:, last_group.par, :, :], beta,
                                    ALU.add).then_inc(last_out_ready, 1)

        @block.gpsimd
        def _(pool):
            def spread_keys(g):
                pool.wait_ge(k_ready, g.value(1))
                if due(g.value(-1)):
                    pool.wait_ge(scored[1], g.value(-1))
                for b in range(2):
                    keys = KT[:, g.slot, b * S:(b + 1) * S].unsqueeze(1).to_broadcast([P, HALF, S])
                    own = own_head[:, :].unsqueeze(2).to_broadcast([P, HALF, S])
                    last = nc.gpsimd.tensor_tensor(Kx[:, g.par, b, :, :], keys, own, ALU.mult)
                last.then_inc(k_spread, 1)

            def root(g):
                pool.wait_ge(var_ready, g.value(1))
                if due(g.value(1 - SLOTS)):
                    pool.wait_ge(norm_ready, g.value(1 - SLOTS))
                nc.gpsimd.tensor_tensor(rstd[:, g.slot:g.slot + 1], var_eps[:, g.slot:g.slot + 1],
                                        neg_half[:, 0:1], ALU.pow).then_inc(rstd_ready, 1)

            def bias_residual(g):
                pool.wait_ge(consts_set, 2)
                if g.layer == 0:
                    pool.wait_ge(state_loaded[g.pair], g.rounds(-SLOTS))
                else:
                    pool.wait_ge(out_ready, g.value(1 - TILES))
                if due(g.value(1 - SLOTS)):
                    pool.wait_ge(z_ready, g.value(1 - SLOTS))
                nc.gpsimd.tensor_tensor(x_bias[:, g.slot, :], state_tile(g), b_o[:, g.layer, :], ALU.add)\
                    .then_inc(res_biased, 1)

            def scale(g):
                if g.n == TILES:
                    pool.wait_ge(loaded_late, LOADED_LATE)
                pool.wait_ge(norm_ready, g.value(1))
                if due(g.value()):
                    pool.wait_ge(out_ready, g.value())
                nc.gpsimd.tensor_tensor(scaled[:, :], normed[:, g.slot, :], ln_g[:, g.layer, :], ALU.mult)\
                    .then_inc(gamma_done, 1)
                pool.wait_ge(consts_set, 2)
                pool.wait_ge(gamma_done, g.value(1))
                nc.gpsimd.tensor_tensor(state_tile(g), scaled[:, :], ln_b[:, g.layer, :], ALU.add)\
                    .then_inc(out_ready, 1)

            def step(i):
                if exists(i):
                    bias_residual(i)
                if exists(i + 2):
                    spread_keys(i + 2)
                if exists(i - 2):
                    root(i - 2)
                if exists(i - 3):
                    scale(i - 3)

            nc.gpsimd.memset(ident[:, :], 0.0).then_inc(consts_zero, 1)
            nc.gpsimd.memset(head_mask[:, :, :], 1.0).then_inc(consts_zero, 1)
            nc.gpsimd.memset(neg_half[:, :], -0.5).then_inc(consts_zero, 1)
            pool.wait_ge(consts_zero, 3)
            nc.gpsimd.affine_select(out=ident[:, :], in_=ident[:, :], compare_op=ALU.not_equal, fill=1.0,
                                    base=0, pattern=[[-1, P]], channel_multiplier=1).then_inc(consts_set, 1)
            nc.gpsimd.affine_select(out=head_mask[:, :, :], in_=head_mask[:, :, :], compare_op=ALU.is_ge,
                                    fill=0.0, base=0, pattern=[[-DH * HALF, 2], [-DH, HALF]],
                                    channel_multiplier=1).then_inc(consts_band, 1)
            pool.wait_ge(consts_band, 1)
            nc.gpsimd.affine_select(out=head_mask[:, :, :], in_=head_mask[:, :, :], compare_op=ALU.is_ge,
                                    fill=0.0, base=DH - 1, pattern=[[DH * HALF, 2], [DH, HALF]],
                                    channel_multiplier=-1).then_inc(consts_band, 1)
            pool.wait_ge(consts_band, 2)
            nc.gpsimd.tensor_tensor(own_head[:, :], head_mask[:, 0, :], head_mask[:, 1, :], ALU.add)\
                .then_inc(consts_set, 1)
            pool.wait_ge(consts_set, 2)
            pool.wait_ge(loaded, LOADED)
            for n in range(-3, 3):
                step(At(n, SLOTS))
            pool.wait_ge(first_norm_loaded, 32)
            walk_tiles(pool, step, 3, G)

            def bias_group(j):
                pool.wait_ge(f_loaded[j.par], j.rounds(-2))
                pool.wait_ge(f_transposed, j.value(1))
                if due(j.value(-1)):
                    pool.wait_ge(f_z_ready, j.value(-1))
                nc.gpsimd.tensor_tensor(f_bias[:, j.par, :, :], f_in[:, j.par, :, :],
                                        b_2[:, :].unsqueeze(1).to_broadcast([P, GROUP, D]), ALU.add)\
                    .then_inc(f_biased, 1)

            def group_root(j):
                pool.wait_ge(f_var_ready, j.value(1))
                if due(j.value(-1)):
                    pool.wait_ge(f_norm_ready, j.value(-1))
                nc.gpsimd.tensor_tensor(f_rstd[:, j.par, :], f_ve[:, j.par, :], neg_half[:, :], ALU.pow)\
                    .then_inc(f_rstd_ready, 1)

            def group_scale(j):
                pool.wait_ge(f_norm_ready, j.value(1))
                if due(j.value()):
                    pool.wait_ge(f_out_ready, j.value())
                gamma = ln_g[:, LAYERS, :].unsqueeze(1).to_broadcast([P, GROUP, D])
                beta = ln_b[:, LAYERS, :].unsqueeze(1).to_broadcast([P, GROUP, D])
                nc.gpsimd.tensor_tensor(f_scaled[:, :, :], f_norm[:, j.par, :, :], gamma, ALU.mult)\
                    .then_inc(f_gamma_done, 1)
                pool.wait_ge(consts_set, 2)
                pool.wait_ge(f_gamma_done, j.value(1))
                nc.gpsimd.tensor_tensor(state_at(j.scaled(GROUP), GROUP), f_scaled[:, :, :], beta, ALU.add)\
                    .then_inc(f_out_ready, 1)

            def group_step(j):
                if group_exists(j + 1):
                    bias_group(j + 1)
                if group_exists(j - 1):
                    group_root(j - 1)
                if group_exists(j - 2):
                    group_scale(j - 2)

            for n in range(3):
                if n < 2:
                    bias_group(At(n, 2))
                step(At(G + n, SLOTS))
            walk_groups(pool, group_step, 1, GROUPS + 1)


def kernel(**inputs):
    import concourse.bacc as bacc
    from concourse.bass_utils import run_bass_kernel_spmd

    nc = bacc.Bacc("TRN2", target_bir_lowering=False, num_devices=1)
    arrays, args = {}, {}
    for name, value in inputs.items():
        v = np.ascontiguousarray(value)
        if v.ndim == 3:
            v = v.reshape(B * S, D)
        arrays[name] = v
        args[name] = nc.dram_tensor(name, v.shape, mybir.dt.from_np(v.dtype), kind="ExternalInput").ap()
    out = nc.dram_tensor("out", (B * S, D), F32, kind="ExternalOutput").ap()
    build(nc, args, out)
    got = run_bass_kernel_spmd(nc, [arrays], core_ids=[0])
    return got.results[0]["out"].reshape(B, S, D)
```
